# Optimizing a Trainium2 kernel written in Bass

```python
import numpy as np
import jax
import jax.numpy as jnp

def _softmax(x, axis=-1):
    return jax.nn.softmax(x, axis=axis)

def _gelu(x):
    return jax.nn.gelu(x, approximate=True)

def _silu(x):
    return jax.nn.silu(x)

def _sigmoid(x):
    return jax.nn.sigmoid(x)

def _layernorm(x, axis=-1, eps=1e-05):
    m = jnp.mean(x, axis=axis, keepdims=True)
    v = jnp.var(x, axis=axis, keepdims=True)
    return (x - m) / jnp.sqrt(v + eps)

def _scatter_add(tgt, idx, src, axis=0):
    return tgt.at[idx].add(src)

def _segment_sum(src, seg, n):
    return jax.ops.segment_sum(src, seg, n)
kernel_name = 'mk_prb_d1_jaxref_r8_c2a424'

def setup_inputs(seed: int=0):
    np.random.seed(seed)
    _w = jnp.asarray

    def _L0_attn_setup():
        import jax, jax.numpy as jnp
        import numpy as np
        HIDDEN = 256
        N_HEADS = 16
        HEAD_DIM = HIDDEN // N_HEADS
        BATCH = 2
        SEQ = 256
        NEG_INF = -1000000000.0
        key = jax.random.key(seed)
        k1, k2, k3 = jax.random.split(key, 3)
        scale = 0.02
        return {'encodings': jax.random.normal(k1, (BATCH, SEQ, HIDDEN), dtype=jnp.float32), 'w_attn': jax.random.normal(k2, (HIDDEN, 3 * HIDDEN), dtype=jnp.float32) * scale, 'b_attn': jnp.zeros((3 * HIDDEN,), dtype=jnp.float32), 'w_proj': jax.random.normal(k3, (HIDDEN, HIDDEN), dtype=jnp.float32) * scale, 'b_proj': jnp.zeros((HIDDEN,), dtype=jnp.float32)}
    _L0_attn_in = _L0_attn_setup()

    def _L0_ffn_setup():
        import jax, jax.numpy as jnp
        import numpy as np
        BLOCK_SIZE = 32
        HIDDEN_SIZE = 256
        MLP_DIM = 2048
        NVFP4_LUT = jnp.array([0.0, 0.5, 1.0, 1.5, 2.0, 3.0, 4.0, 6.0, 0.0, -0.5, -1.0, -1.5, -2.0, -3.0, -4.0, -6.0], dtype=jnp.float32)

        def dequant_nvfp4(W_packed, scales, block=BLOCK_SIZE):
            N = W_packed.shape[0]
            low = W_packed & 15
            high = W_packed >> 4 & 15
            idx = jnp.stack([low, high], axis=-1).reshape(N, -1)
            vals = NVFP4_LUT[idx]
            K = vals.shape[1]
            vals = vals.reshape(N, K // block, block) * scales[:, :, None]
            return vals.reshape(N, K)
        key = jax.random.key(seed)
        ks = jax.random.split(key, 7)
        x = jax.random.normal(ks[0], (4, 32, HIDDEN_SIZE), dtype=jnp.float32)
        gate_W_packed = jax.random.randint(ks[1], (MLP_DIM, HIDDEN_SIZE // 2), 0, 32, dtype=jnp.int32)
        gate_scales = jax.random.uniform(ks[2], (MLP_DIM, HIDDEN_SIZE // BLOCK_SIZE), dtype=jnp.float32) * 0.1 + 0.001
        up_W_packed = jax.random.randint(ks[3], (MLP_DIM, HIDDEN_SIZE // 2), 0, 32, dtype=jnp.int32)
        up_scales = jax.random.uniform(ks[4], (MLP_DIM, HIDDEN_SIZE // BLOCK_SIZE), dtype=jnp.float32) * 0.1 + 0.001
        down_W_packed = jax.random.randint(ks[5], (HIDDEN_SIZE, MLP_DIM // 2), 0, 32, dtype=jnp.int32)
        down_scales = jax.random.uniform(ks[6], (HIDDEN_SIZE, MLP_DIM // BLOCK_SIZE), dtype=jnp.float32) * 0.1 + 0.001
        return {'x': x, 'gate_W_packed': gate_W_packed, 'gate_scales': gate_scales, 'up_W_packed': up_W_packed, 'up_scales': up_scales, 'down_W_packed': down_W_packed, 'down_scales': down_scales}
    _L0_ffn_in = _L0_ffn_setup()
    _d = {'L0_attn_encodings': _L0_attn_in['encodings'], 'L0_attn_w_attn': _L0_attn_in['w_attn'], 'L0_attn_b_attn': _L0_attn_in['b_attn'], 'L0_attn_w_proj': _L0_attn_in['w_proj'], 'L0_attn_b_proj': _L0_attn_in['b_proj'], 'L0_ffn_gate_W_packed': _L0_ffn_in['gate_W_packed'], 'L0_ffn_gate_scales': _L0_ffn_in['gate_scales'], 'L0_ffn_up_W_packed': _L0_ffn_in['up_W_packed'], 'L0_ffn_up_scales': _L0_ffn_in['up_scales'], 'L0_ffn_down_W_packed': _L0_ffn_in['down_W_packed'], 'L0_ffn_down_scales': _L0_ffn_in['down_scales']}
    _x0 = _d['L0_attn_encodings']
    _d['L0_attn_encodings'] = jax.random.normal(jax.random.fold_in(jax.random.key(seed), 1), (4, 1024, 256), dtype=_x0.dtype)
    del _x0
    return _d

def reference(L0_attn_encodings, L0_attn_w_attn, L0_attn_b_attn, L0_attn_w_proj, L0_attn_b_proj, L0_ffn_gate_W_packed, L0_ffn_gate_scales, L0_ffn_up_W_packed, L0_ffn_up_scales, L0_ffn_down_W_packed, L0_ffn_down_scales):

    def _L0_attn_ref(encodings, w_attn, b_attn, w_proj, b_proj):
        import jax, jax.numpy as jnp
        import numpy as np
        HIDDEN = 256
        N_HEADS = 16
        HEAD_DIM = HIDDEN // N_HEADS
        BATCH = 2
        SEQ = 256
        NEG_INF = -1000000000.0
        B, S, H = encodings.shape
        qkv = encodings @ w_attn + b_attn
        q, k, v = jnp.split(qkv, 3, axis=-1)
        split = lambda x: x.reshape(B, S, N_HEADS, HEAD_DIM).transpose(0, 2, 1, 3)
        q, k, v = (split(q), split(k), split(v))
        scores = jnp.einsum('bhqd,bhkd->bhqk', q, k) / jnp.sqrt(jnp.asarray(HEAD_DIM, dtype=q.dtype))
        causal = jnp.tril(jnp.ones((S, S), dtype=bool))
        scores = jnp.where(causal, scores, NEG_INF)
        attn_weights = jax.nn.softmax(scores, axis=-1)
        attn_output = jnp.einsum('bhqk,bhkd->bhqd', attn_weights, v)
        attn_output = attn_output.transpose(0, 2, 1, 3).reshape(B, S, H)
        return attn_output @ w_proj + b_proj

    def _L0_ffn_ref(x, gate_W_packed, gate_scales, up_W_packed, up_scales, down_W_packed, down_scales):
        import jax, jax.numpy as jnp
        import numpy as np
        BLOCK_SIZE = 32
        HIDDEN_SIZE = 256
        MLP_DIM = 2048
        NVFP4_LUT = jnp.array([0.0, 0.5, 1.0, 1.5, 2.0, 3.0, 4.0, 6.0, 0.0, -0.5, -1.0, -1.5, -2.0, -3.0, -4.0, -6.0], dtype=jnp.float32)

        def dequant_nvfp4(W_packed, scales, block=BLOCK_SIZE):
            N = W_packed.shape[0]
            low = W_packed & 15
            high = W_packed >> 4 & 15
            idx = jnp.stack([low, high], axis=-1).reshape(N, -1)
            vals = NVFP4_LUT[idx]
            K = vals.shape[1]
            vals = vals.reshape(N, K // block, block) * scales[:, :, None]
            return vals.reshape(N, K)
        B, S, H = x.shape
        xt = x.reshape(B * S, H)
        Wg = dequant_nvfp4(gate_W_packed, gate_scales)
        Wu = dequant_nvfp4(up_W_packed, up_scales)
        Wd = dequant_nvfp4(down_W_packed, down_scales)
        gate = jnp.einsum('th,nh->tn', xt, Wg)
        up = jnp.einsum('th,nh->tn', xt, Wu)
        gelu = jnp.tanh(0.7978845608028654 * (gate + 0.044715 * gate ** 3)) * gate * 0.5 + gate * 0.5
        inter = gelu * up
        out = jnp.einsum('tn,hn->th', inter, Wd)
        return out.reshape(B, S, H)
    x = L0_attn_encodings
    xn = _layernorm(x, axis=-1)
    x = x + _L0_attn_ref(xn, L0_attn_w_attn, L0_attn_b_attn, L0_attn_w_proj, L0_attn_b_proj) + _L0_ffn_ref(xn, L0_ffn_gate_W_packed, L0_ffn_gate_scales, L0_ffn_up_W_packed, L0_ffn_up_scales, L0_ffn_down_W_packed, L0_ffn_down_scales)
    return x

_drawn_inputs = setup_inputs


def setup_inputs(seed=0):
    import zlib

    import numpy as np

    out = dict(_drawn_inputs(seed))
    spreads = {'L0_attn_b_attn': (0.0, 0.8), 'L0_attn_b_proj': (0.0, 0.8)}
    factors = {'L0_attn_w_attn': 8.0, 'L0_attn_w_proj': 8.0}
    for name, (base, spread) in spreads.items():
        noise = np.random.default_rng([zlib.crc32(name.encode()), seed]).standard_normal(out[name].shape)
        drawn = base * np.exp(spread * noise) if base else spread * noise
        out[name] = jnp.asarray(drawn.astype(out[name].dtype))
    for name, factor in factors.items():
        out[name] = (out[name] * factor).astype(out[name].dtype)
    return out
```

```python
import concourse.bass as bass
from concourse import mybir
from contextlib import ExitStack

f32 = mybir.dt.float32
f32r = mybir.dt.float32r
bf16 = mybir.dt.bfloat16
i32 = mybir.dt.int32
fp8 = mybir.dt.float8e4
ALU = mybir.AluOpType
ACT = mybir.ActivationFunctionType
AX = mybir.AxisListType

P = 128
B, S, H = 4, 1024, 256
NH, HD = 16, 16
F = 2048
KT = H // P
NT = F // P
TT = S // P
UNIT = 256
NU = S // UNIT
PAIRS = NT // 2
NI = NU * PAIRS
GH = 4
NG = NH // GH
BLK = 32
TERMS_Q = (0, 0, 0, 1, 1, 2)
TERMS_K = (0, 1, 2, 0, 1, 0)
NTERM = len(TERMS_Q)
KS_ROWS = NTERM * HD
KM_ROWS = KS_ROWS + 3
LOWEST = -3.0e38
EPS = 1e-5
PASSES = ((0, 0), (0, 1), (1, 0))


def sequence_steps():
    steps = []
    slots = []
    for i in range(NI):
        slots.append([("up", i)] if i == 0 else [("split", i - 1), ("up", i)])
        slots.append([("gate", i)] + ([("down", i - 1)] if i else []))
        if i and i % PAIRS == 0:
            slots[-1].append(("unit", i // PAIRS - 1))
    slots.reverse()

    def ffn(n):
        for _ in range(n):
            steps.extend(slots.pop())

    steps += [("qk", 0, n) for n in range(4)]
    steps += [("spill", 0), ("stage", 0)]
    steps += [("v", j) for j in range(TT)]
    ffn(4)
    for g in range(NG):
        for h in range(GH):
            for part in range(2):
                steps.append(("scores", g, h, part))
                ffn(1)
        steps.append(("maxima", g))
        ffn(1)
        steps.append(("max_rows", g))
        if g == 1:
            steps += [("qk", 1, n) for n in range(4)] + [("spill", 1)]
            ffn(2)
        ffn(1)
        for t in range(12):
            steps.append(("weights", g, t))
            if t == 5:
                steps.append(("heads_out", g, 0))
            if t in (3, 8):
                ffn(1)
        if g < NG - 1:
            steps.append(("stage", g + 1))
        steps.append(("weights_end", g))
        ffn(1)
        steps.append(("heads_out", g, 1))
        ffn(1)
    ffn(len(slots))
    steps += [("split", NI - 1), ("down", NI - 1), ("unit", NU - 1)]
    steps += [("project", j) for j in range(TT)]
    return steps


def score_chunks(part):
    out = []
    for qb in range(TT):
        for k0 in range(0, (qb + 1) * P, 512):
            out.append((qb, k0, min(k0 + 512, (qb + 1) * P)))
    half = len(out) // 2
    return out[:half] if part == 0 else out[half:]


def weight_chunk(t):
    half, j = (0, t) if t < 4 else (1, t - 4)
    diagonal = j >= 4 * half
    return half, j, P * (j - 4 * half) if diagonal else 0, diagonal


def build(nc, x_in, w_attn, b_attn, w_proj, b_proj, gate_w, gate_s, up_w, up_s, down_w, down_s, out):
    STEPS = sequence_steps()

    ring_first, n = {}, 0
    for s in STEPS:
        uses = {"qk": 1, "v": 1, "scores": 6, "max_rows": 1, "weights": GH, "project": 1}.get(s[0], 0)
        if uses:
            ring_first[s] = n
            n += uses
    RING = n
    assert RING % 2 == 0

    top = ExitStack()
    with top:
        def sb(name, shape, dt, where=None):
            return (where or top).enter_context(nc.sbuf_tensor(name, shape, dt))

        def sem(name, where=None):
            return (where or top).enter_context(nc.semaphore(name))

        WG = sb("WG", [P, 2, KT, F], f32r)
        WU = sb("WU", [P, 2, KT, F], f32r)
        WD = sb("WD", [P, 2, NT, H], f32r)
        WA = sb("WA", [P, 2, KT, 3 * H], f32r)
        WP = sb("WP", [P, KT, H], f32)
        bqk = sb("bqk", [P, 4], f32)
        bv = sb("bv", [P, H], f32)
        bp = sb("bp", [P, H], f32)
        ident = sb("ident", [P, P], f32)
        causal = sb("causal", [P, P], f32)
        banks = [top.enter_context(nc.psum_tensor(f"bank{i}", [P, 512], f32)) for i in range(8)]
        qk_dram = nc.dram_tensor("qk_parts", (2, 2, P, 3, S), bf16, kind="Internal").ap()
        xn_dram = nc.dram_tensor("xn_parts", (B, NU, P, 2, KT, UNIT), f32, kind="Internal").ap()

        setup_phase(nc, sem, sb, banks, locals())
        main_phase(nc, sem, sb, banks, locals(), STEPS, ring_first, RING)


def setup_phase(nc, sem, sb, banks, T):
    WG, WU, WD, WA, WP = T["WG"], T["WU"], T["WD"], T["WA"], T["WP"]
    ident, causal, xn_dram = T["ident"], T["causal"], T["xn_dram"]
    NX = B * S // P
    NC = 12
    CW = 512
    with ExitStack() as own:
        X = sb("X", [P, NX, H], f32, own)
        stats = sb("stats", [P, NX, 6], f32, own)
        mv = sb("mv", [P, NX, 2], f32, own)
        rs = sb("rs", [P, 4, NX], f32, own)
        XS = sb("XS", [P, 2, 2, KT, 512], f32r, own)
        PK = sb("PK", [P, 2, CW], i32, own)
        CODE = sb("CODE", [P, 4, CW], i32, own)
        WF = sb("WF", [P, 2, 2 * CW], f32, own)
        SC = sb("SC", [P, 3, P], f32, own)
        WT = sb("WT", [P, KT, 3 * H], f32, own)

        x_loaded = [sem(f"x_loaded{b}", own) for b in range(B)]
        wa_loaded, wp_loaded, bias_loaded, sc_loaded = (sem(n, own) for n in ("wa_loaded", "wp_loaded", "bias_loaded", "sc_loaded"))
        pk_loaded = [sem(f"pk_loaded{i}", own) for i in range(2)]
        consts_made = sem("consts_made", own)
        dve_step = sem("dve_step", own)
        var_ready, root_ready, xn_ready = (sem(n, own) for n in ("var_ready", "root_ready", "xn_ready"))
        xt_full, x_hi, x_lo = (sem(n, own) for n in ("xt_full", "x_hi", "x_lo"))
        xs_stored = [sem(f"xs_stored{i}", own) for i in range(2)]
        wa_hi, code_read, wf_ready, wt_full, w_hi, w_lo = (sem(n, own) for n in ("wa_hi", "code_read", "wf_ready", "wt_full", "w_hi", "w_lo"))
        block = own.enter_context(nc.Block())

        def packed(c):
            if c < 8:
                w = T["gate_w"] if c < 4 else T["up_w"]
                return w[(c % 4) * 512:(c % 4 + 1) * 512, :].rearrange("(i p) w -> p i w", p=P)
            c -= 8
            return T["down_w"][(c // 2) * P:(c // 2 + 1) * P, (c % 2) * CW:(c % 2 + 1) * CW]

        def weight_dest(c, part, k):
            if c < 8:
                return (WG if c < 4 else WU)[:, part, k, (c % 4) * 512:(c % 4 + 1) * 512]
            c -= 8
            nt = (c % 2) * 8 + 4 * k
            return WD[:, part, nt:nt + 4, (c // 2) * P:(c // 2 + 1) * P]

        def bank_view(bank, c):
            return bank[:, :] if c < 8 else bank[:, :].rearrange("p (n h) -> p n h", h=P)

        @block.sync
        def _(sp):
            for b in range(B):
                sp.dma_start(X[:, b * TT:(b + 1) * TT, :],
                             T["x_in"][b].rearrange("(t p) h -> p t h", p=P)).then_inc(x_loaded[b], 16)
                if b == 0:
                    sp.dma_start(SC[:, 0, :].rearrange("p (t s) -> p t s", s=8),
                                 T["gate_s"].rearrange("(t p) s -> p t s", p=P)).then_inc(sc_loaded, 16)
                    sp.dma_start(SC[:, 1, :].rearrange("p (t s) -> p t s", s=8),
                                 T["up_s"].rearrange("(t p) s -> p t s", p=P)).then_inc(sc_loaded, 16)
                    sp.dma_start(SC[:, 2, :].rearrange("p (t s) -> p t s", s=64),
                                 T["down_s"].rearrange("(t p) s -> p t s", p=P)).then_inc(sc_loaded, 16)
                    sp.dma_start(WT[:], T["w_attn"].rearrange("(k p) n -> p k n", p=P)).then_inc(wa_loaded, 16)
                    sp.dma_start(WP[:], T["w_proj"].rearrange("(k p) n -> p k n", p=P)).then_inc(wp_loaded, 16)
                    for i in range(2):
                        sp.dma_start(PK[:, i, :].rearrange("p (i w) -> p i w", w=P), packed(i)).then_inc(pk_loaded[i], 16)
                    sp.dma_start(T["bqk"][:], T["b_attn"][0:2 * H].rearrange("(t p) -> p t", p=P),
                                 allow_slow_non_contiguous=True).then_inc(bias_loaded, 16)
                    sp.dma_start(T["bv"][:], T["b_attn"][2 * H:3 * H].partition_broadcast(P)).then_inc(bias_loaded, 16)
                    sp.dma_start(T["bp"][:], T["b_proj"].partition_broadcast(P)).then_inc(bias_loaded, 16)
            for c in range(B * S // 512):
                sp.wait_ge(x_lo, 2 * c + 2)
                for u in range(2):
                    sp.dma_start(xn_dram[c // 2, 2 * (c % 2) + u],
                                 XS[:, c % 2, :, :, u * UNIT:(u + 1) * UNIT].bitcast(f32)).then_inc(xs_stored[c % 2], 16)
            for c in range(2, NC):
                sp.wait_ge(code_read, c - 1)
                dst = PK[:, c % 2, :]
                if c < 8:
                    dst = dst.rearrange("p (i w) -> p i w", w=P)
                sp.dma_start(dst, packed(c)).then_inc(pk_loaded[c % 2], 16)
            for i in range(2):
                sp.wait_ge(xs_stored[i], 16 * B * S // 512)
            sp.wait_ge(wp_loaded, 16)
            sp.wait_ge(bias_loaded, 48)

        @block.gpsimd
        def _(pool):
            nc.gpsimd.memset(ident[:], 0.0).then_inc(consts_made, 1)
            nc.gpsimd.memset(causal[:], 0.0).then_inc(consts_made, 1)
            pool.wait_ge(consts_made, 2)
            nc.gpsimd.affine_select(out=ident[:], in_=ident[:], compare_op=ALU.not_equal, fill=1.0, base=0,
                                    pattern=[[-1, P]], channel_multiplier=1).then_inc(consts_made, 1)
            nc.gpsimd.affine_select(out=causal[:], in_=causal[:], compare_op=ALU.is_ge, fill=LOWEST, base=0,
                                    pattern=[[-1, P]], channel_multiplier=1).then_inc(consts_made, 1)

        @block.vector
        def _(dve):
            done = [0]

            def link(ins):
                ins.then_inc(dve_step, 1)
                done[0] += 1
                dve.wait_ge(dve_step, done[0])

            def lo_parts(c):
                for k in range(KT):
                    dve.wait_ge(x_hi, 2 * c + k + 1)
                    if c >= 2:
                        dve.wait_ge(xs_stored[c % 2], 32 * (c // 2))
                    nc.vector.tensor_tensor(XS[:, c % 2, 1, k, :], banks[4 + 2 * (c % 2) + k][:, :],
                                            XS[:, c % 2, 0, k, :].bitcast(f32), ALU.subtract).then_inc(x_lo, 1)

            for b in range(B):
                dve.wait_ge(x_loaded[b], 16)
                own_tiles = slice(b * TT, (b + 1) * TT)
                for t in range(b * TT, (b + 1) * TT):
                    last = nc.vector.bn_stats(stats[:, t, :], X[:, t, :])
                link(last)
                for t in range(b * TT, (b + 1) * TT):
                    last = nc.vector.bn_aggr(mv[:, t, :], stats[:, t, :])
                link(last)
                nc.vector.tensor_scalar(rs[:, 0, own_tiles], mv[:, own_tiles, 1], EPS, None,
                                        ALU.add).then_inc(var_ready, 1)
                dve.wait_ge(var_ready, b + 1)
                dve.wait_ge(root_ready, b + 1)
                link(nc.vector.reciprocal(rs[:, 2, own_tiles], rs[:, 1, own_tiles]))
                link(nc.vector.tensor_tensor(rs[:, 3, own_tiles], rs[:, 2, own_tiles], rs[:, 2, own_tiles], ALU.mult))
                link(nc.vector.tensor_tensor(rs[:, 3, own_tiles], rs[:, 3, own_tiles], rs[:, 0, own_tiles], ALU.mult))
                link(nc.vector.tensor_scalar(rs[:, 3, own_tiles], rs[:, 3, own_tiles], -0.5, 1.5, ALU.mult, ALU.add))
                link(nc.vector.tensor_tensor(rs[:, 2, own_tiles], rs[:, 2, own_tiles], rs[:, 3, own_tiles], ALU.mult))
                for t in range(b * TT, (b + 1) * TT):
                    nc.vector.tensor_scalar(X[:, t, :], X[:, t, :], mv[:, t, 0:1], rs[:, 2, t:t + 1],
                                            ALU.subtract, ALU.mult).then_inc(xn_ready, 1)
                for c in (2 * b, 2 * b + 1):
                    lo_parts(c)
            dve.wait_ge(wa_hi, 1)
            nc.vector.tensor_tensor(WA[:, 1], WT[:], WA[:, 0].bitcast(f32), ALU.subtract)
            dve.wait_ge(sc_loaded, 48)
            nc.vector.tensor_scalar(SC[:, 0:2], SC[:, 0:2], 64.0, None, ALU.mult)
            link(nc.vector.tensor_scalar(SC[:, 2], SC[:, 2], 32.0, None, ALU.mult))

            def w_lo_parts(c):
                for k in range(2):
                    dve.wait_ge(w_hi, 2 * c + k + 1)
                    nc.vector.tensor_tensor(weight_dest(c, 1, k), bank_view(banks[2 * (c % 2) + k], c),
                                            weight_dest(c, 0, k).bitcast(f32), ALU.subtract).then_inc(w_lo, 1)

            for c in range(NC):
                dve.wait_ge(pk_loaded[c % 2], 16 * (c // 2 + 1))
                src = PK[:, c % 2, :]
                for i, (shift, mask) in enumerate(((2, 0x1C), (4, 0x80), (6, 0x1C00), (8, 0x8000))):
                    last = nc.vector.tensor_scalar(CODE[:, i, :], src, shift, mask, ALU.logical_shift_left, ALU.bitwise_and)
                last.then_inc(code_read, 1)
                dve.wait_ge(code_read, c + 1)
                link(nc.vector.tensor_tensor(CODE[:, 0:2, :], CODE[:, 0:2, :], CODE[:, 2:4, :], ALU.bitwise_or))
                link(nc.vector.tensor_tensor(CODE[:, 0, :], CODE[:, 0, :], CODE[:, 1, :], ALU.bitwise_or))
                if c >= 2:
                    dve.wait_ge(wt_full, 2 * c - 2)
                which, first = (c // 4, (c % 4) * 32) if c < 8 else (2, ((c - 8) // 2) * 64 + (c % 2) * 32)
                scale = SC[:, which, first:first + 32].unsqueeze(2).unsqueeze(3).to_broadcast([P, 32, BLK // 2, 2])
                code = CODE[:, 0, :].bitcast(fp8).rearrange("p (b w c) -> p b w c", b=32, c=4)[:, :, :, 0:2]
                nc.vector.tensor_tensor(WF[:, c % 2, :].rearrange("p (b w c) -> p b w c", b=32, c=2),
                                        code, scale, ALU.mult).then_inc(wf_ready, 1)
                dve.wait_ge(wf_ready, c + 1)
                if c:
                    w_lo_parts(c - 1)
            w_lo_parts(NC - 1)

        @block.scalar
        def _(act):
            def hi_parts(c):
                for k in range(KT):
                    act.wait_ge(xt_full, 2 * c + k + 1)
                    if c >= 2:
                        act.wait_ge(xs_stored[c % 2], 32 * (c // 2))
                    nc.scalar.activation(XS[:, c % 2, 0, k, :], banks[4 + 2 * (c % 2) + k][:, :],
                                         ACT.Copy).then_inc(x_hi, 1)

            for b in range(B):
                act.wait_ge(var_ready, b + 1)
                own_tiles = slice(b * TT, (b + 1) * TT)
                nc.scalar.activation(rs[:, 1, own_tiles], rs[:, 0, own_tiles], ACT.Sqrt).then_inc(root_ready, 1)
                for c in (2 * b, 2 * b + 1):
                    hi_parts(c)
            act.wait_ge(wa_loaded, 16)
            nc.scalar.activation(WA[:, 0], WT[:], ACT.Copy).then_inc(wa_hi, 1)
            for c in range(NC):
                for k in range(2):
                    act.wait_ge(wt_full, 2 * c + k + 1)
                    nc.scalar.activation(weight_dest(c, 0, k), bank_view(banks[2 * (c % 2) + k], c),
                                         ACT.Copy).then_inc(w_hi, 1)

        @block.tensor
        def _(pe):
            pe.wait_ge(consts_made, 4)
            for c in range(B * S // 512):
                for k in range(KT):
                    if c >= 2:
                        pe.wait_ge(x_lo, 2 * (c - 2) + k + 1)
                    for i in range(4):
                        t = 4 * c + i
                        pe.wait_ge(xn_ready, t + 1)
                        last = nc.tensor.transpose(banks[4 + 2 * (c % 2) + k][:, i * P:(i + 1) * P],
                                                   X[:, t, k * P:(k + 1) * P], ident[:])
                    last.then_inc(xt_full, 1)
            for c in range(NC):
                pe.wait_ge(wf_ready, c + 1)
                for k in range(2):
                    if c >= 2:
                        pe.wait_ge(w_lo, 2 * (c - 2) + k + 1)
                    for i in range(4):
                        col = (i * KT + k) * P if c < 8 else (4 * k + i) * P
                        last = nc.tensor.transpose(banks[2 * (c % 2) + k][:, i * P:(i + 1) * P],
                                                   WF[:, c % 2, col:col + P], ident[:])
                    last.then_inc(wt_full, 1)


def main_phase(nc, sem, sb, banks, T, STEPS, ring_first, RING):
    WG, WU, WD, WA, WP = T["WG"], T["WU"], T["WD"], T["WA"], T["WP"]
    ident, causal, xn_dram, qk_dram = T["ident"], T["causal"], T["xn_dram"], T["qk_dram"]
    acc, gate_b, up_b, ring, pv = banks[0], banks[1:3], banks[3:5], banks[5:7], banks[7]
    with ExitStack() as own:
        xT = sb("xT", [P, 2, KT, S], f32r, own)
        res = sb("res", [P, TT, H], f32, own)
        QF = sb("QF", [P, 2, 512], f32, own)
        PT = sb("PT", [P, 2, 3, S], bf16, own)
        QS = sb("QS", [P, GH, S], bf16, own)
        KS = sb("KS", [P, GH, S], bf16, own)
        V1 = sb("V1", [P, TT, NH, HD + 1], f32, own)
        junk = sb("junk", [P, 2, P], f32, own)
        tick = sb("tick", [P, 4], f32, own)
        carry = sb("carry", [1, 2 * GH + 1], f32, own)
        MX = sb("MX", [P, GH * TT, 3], f32, own)
        NM = sb("NM", [P, GH * TT], f32, own)
        MR = sb("MR", [GH * TT, P], f32, own)
        MT = sb("MT", [GH * TT, 3, P], bf16, own)
        PR = sb("PR", [P, 2 * GH, 512], f32, own)
        OT = sb("OT", [P, 512], f32, own)
        RC = sb("RC", [P, 16], f32, own)
        OD = sb("OD", [P, 2, 512], f32, own)
        OP = sb("OP", [P, KT, S], f32, own)
        A = sb("A", [P, 2, 512], f32, own)
        HI = sb("HI", [P, 2, 512], f32r, own)
        LO = sb("LO", [P, 2, 512], f32r, own)

        made = sem("made", own)
        xt_ready = [sem(f"xt_ready{u}", own) for u in range(NU)]
        x_ready, bias_added = sem("x_ready", own), sem("bias_added", own)
        ring_full = [sem(f"ring_full{i}", own) for i in range(2)]
        ring_free = [sem(f"ring_free{i}", own) for i in range(2)]
        part1, rest1, part2, part3 = (sem(n, own) for n in ("part1", "rest1", "part2", "part3"))
        staged = sem("staged", own)
        spilled = [sem(f"spilled{m}", own) for m in range(2)]
        maxima_done, mr1, mr2, mr3, rows_split, rows_ready = (
            sem(n, own) for n in ("maxima_done", "mr1", "mr2", "mr3", "rows_split", "rows_ready"))
        masked, weights_used = sem("masked", own), sem("weights_used", own)
        pv_read, o_step, o_ready = sem("pv_read", own), sem("o_step", own), sem("o_ready", own)
        packed = [sem(f"packed{i}", own) for i in range(2)]
        gate_full, up_full, squared, cubed, tanhed, gelued, product, hi_done, lo_done, down_done, acc_read = (
            sem(n, own) for n in ("gate_full", "up_full", "squared", "cubed", "tanhed", "gelued", "product",
                                  "hi_done", "lo_done", "down_done", "acc_read"))
        carried, carried_out = sb("carried", [1, 2], f32, own), sem("carried_out", own)
        finished, stored = sem("finished", own), sem("stored", own)
        block = own.enter_context(nc.Block())

        qk_index = {("qk", m, n): 4 * m + n for m in range(2) for n in range(4)}
        diagonals = [t for t in range(12) if weight_chunk(t)[3]]
        NQ, NW, NO = 8, NG * 12, NG * 2

        def wait(eng, s, b, per, k):
            eng.wait_ge(s, b * per + (max(k, 0) + 1))

        def wait_ring_full(eng, b, use):
            wait(eng, ring_full[use % 2], b, RING // 2, use // 2 + 1)

        def wait_ring_free(eng, b, use):
            wait(eng, ring_free[use % 2], b, RING // 2, use // 2)

        def wait_ring_read(eng, b, use):
            wait(eng, ring_free[use % 2], b, RING // 2, use // 2 + 1)

        @block.sync
        def _(sp):
            counted = [x_ready, bias_added, part1, rest1, part2, part3, staged, maxima_done, mr1, mr2, mr3, rows_split,
                       rows_ready, masked, weights_used, pv_read, o_step, o_ready, gate_full, up_full, squared, cubed,
                       tanhed, gelued, product, hi_done, lo_done, down_done, acc_read, finished, stored]
            for s in counted + xt_ready + ring_full + ring_free + spilled + packed:
                sp.sem_inc(s, 1)
            with sp.Fori(0, B) as b:
                for s in STEPS:
                    if s[0] == "spill":
                        m = s[1]
                        wait(sp, part3, b, NQ, 4 * m + 4)
                        for which in range(2):
                            sp.dma_start(qk_dram[m, which], PT[:, which]).then_inc(spilled[m], 16)
                    elif s[0] == "stage":
                        g = s[1]
                        m, p0 = g // 2, (g % 2) * GH * HD
                        if g == 0:
                            wait(sp, spilled[0], b, 32, 32)
                        else:
                            wait_ring_full(sp, b, ring_first["weights", g - 1, 11] + GH - 1)
                        q_dram, k_dram = (qk_dram[m, which, p0:p0 + GH * HD].rearrange("(h r) c t -> c r h t", r=HD)
                                          for which in range(2))
                        row = 0
                        for part in range(3):
                            for _ in range(3 - part):
                                sp.dma_start(QS[row:row + HD], q_dram[part]).then_inc(staged, 16)
                                row += HD
                        row = 0
                        for count in range(3, 0, -1):
                            for part in range(count):
                                sp.dma_start(KS[row:row + HD], k_dram[part]).then_inc(staged, 16)
                                row += HD
                    elif s[0] == "max_rows":
                        wait(sp, rows_split, b, NG, s[1] + 1)
                        for c in range(3):
                            sp.dma_start(QS[KS_ROWS + c:KS_ROWS + c + 1].rearrange("o h (q t) -> o (h q) t", t=P),
                                         MT[:, c, :]).then_inc(rows_ready, 16)
                    elif s[0] == "heads_out":
                        g, half = s[1], s[2]
                        wait(sp, o_ready, b, NO, 2 * g + half + 1)
                        for h in range(GH):
                            row = ((g % 2) * GH + h) * HD
                            if (g, half, h) == (1, 0, 1):
                                wait(sp, spilled[1], b, 32, 32)
                            sp.dma_start(OP[row:row + HD, g // 2, half * 512:(half + 1) * 512],
                                         OD[32 * h:32 * h + HD, half, :]).then_inc(packed[half], 16)
                    elif s[0] == "project" and s[1] % 4 == 3:
                        j = s[1] - 3
                        wait(sp, finished, b, TT, j + 4)
                        sp.dma_start(carried[:, j // 4:j // 4 + 1], res[0:1, j, 0:1]).then_inc(carried_out, 16)
                        sp.dma_start(T["out"][b].rearrange("(t p) h -> p t h", p=P)[:, j:j + 4, :],
                                     res[:, j:j + 4, :]).then_inc(stored, 16)
            sp.wait_ge(stored, B * 32 + 1)
            sp.wait_ge(carried_out, B * 32)

        @block.gpsimd
        def _(pool):
            nc.gpsimd.memset(carry[:], 0.0).then_inc(made, 1)
            with pool.Fori(0, B) as b:
                for s in STEPS:
                    if s[0] == "qk":
                        n = qk_index[s]
                        wait(pool, part2, b, NQ, n + 1)
                        which, c = (s[2] // 2) % 2, s[2] % 2
                        nc.gpsimd.tensor_tensor(PT[:, which, 2, c * 512:(c + 1) * 512], QF[:, n % 2, :],
                                                PT[:, which, 1, c * 512:(c + 1) * 512], ALU.subtract).then_inc(part3, 1)
                    elif s == ("v", TT - 1):
                        wait(pool, x_ready, b, 16, 16)
                        nc.gpsimd.tensor_tensor(res[:], res[:], T["bp"][:].unsqueeze(1).to_broadcast([P, TT, H]),
                                                ALU.add).then_inc(bias_added, 1)
                    elif s[0] == "weights":
                        g, t = s[1], s[2]
                        half, j, off, diagonal = weight_chunk(t)
                        if diagonal:
                            for h in range(GH):
                                wait_ring_read(pool, b, ring_first[s] + h)
                                at = 1 + (t % 2) * GH + h
                                nc.gpsimd.tensor_tensor(carry[:, at:at + 1], carry[:, 0:1], carry[:, 0:1],
                                                        ALU.add)
                                blk = PR[:, (t % 2) * GH + h, 0:P]
                                nc.gpsimd.affine_select(out=blk, in_=blk, compare_op=ALU.is_ge, fill=0.0, base=0,
                                                        pattern=[[1, P]], channel_multiplier=-1).then_inc(masked, 1)
                    elif s[0] == "split":
                        i = s[1]
                        wait(pool, hi_done, b, NI, i + 1)
                        wait(pool, down_done, b, NI, i - 1)
                        nc.gpsimd.tensor_tensor(LO[:, i % 2, :], A[:, i % 2, :], HI[:, i % 2, :].bitcast(f32),
                                                ALU.subtract).then_inc(lo_done, 1)

        @block.scalar
        def _(act):
            with act.Fori(0, B) as b:
                wait(act, up_full, b, NI, 0)
                for u in range(NU):
                    act.dma_start(xT[:, :, :, u * UNIT:(u + 1) * UNIT].bitcast(f32), xn_dram[b, u]).then_inc(xt_ready[u], 16)
                for s in STEPS:
                    if s[0] == "qk":
                        n = qk_index[s]
                        which, c = (s[2] // 2) % 2, s[2] % 2
                        cols = slice(c * 512, (c + 1) * 512)
                        wait_ring_read(act, b, ring_first[s])
                        if s[2] == 0:
                            wait(act, spilled[1 - s[1]], b, 32, 32 * s[1])
                        nc.scalar.activation(PT[:, which, 0, cols], QF[:, n % 2, :], ACT.Copy).then_inc(part1, 1)
                        wait(act, rest1, b, NQ, n + 1)
                        nc.scalar.activation(PT[:, which, 1, cols], QF[:, n % 2, :], ACT.Copy).then_inc(part2, 1)
                    elif s == ("v", TT - 1):
                        wait(act, stored, b, 32, 0)
                        act.dma_start(res[:], T["x_in"][b].rearrange("(t p) h -> p t h", p=P)).then_inc(x_ready, 16)
                    elif s[0] == "weights":
                        g, t = s[1], s[2]
                        half, j, off, diagonal = weight_chunk(t)
                        wait(act, weights_used, b, NW, g * 12 + t - 1)
                        for h in range(GH):
                            use = ring_first[s] + h
                            wait_ring_full(act, b, use)
                            nc.scalar.activation(PR[:, (t % 2) * GH + h, 0:512 - off], ring[use % 2][:, 0:512 - off],
                                                 ACT.Exp, scale=0.25).then_inc(ring_free[use % 2], 1)
                    elif s[0] == "up":
                        i = s[1]
                        wait(act, gate_full, b, NI, i + 1)
                        wait(act, lo_done, b, NI, i - 1)
                        nc.scalar.activation(A[:, i % 2, :], gate_b[i % 2][:, :], ACT.Square,
                                             scale=0.044715 ** 0.5).then_inc(squared, 1)
                    elif s[0] == "gate":
                        i = s[1]
                        wait(act, cubed, b, NI, i + 1)
                        nc.scalar.activation(A[:, i % 2, :], A[:, i % 2, :], ACT.Tanh,
                                             scale=0.7978845608028654).then_inc(tanhed, 1)
                    elif s[0] == "split":
                        i = s[1]
                        wait(act, product, b, NI, i + 1)
                        wait(act, down_done, b, NI, i - 1)
                        nc.scalar.activation(HI[:, i % 2, :], A[:, i % 2, :], ACT.Copy).then_inc(hi_done, 1)

        @block.vector
        def _(dve):
            nc.vector.memset(V1[:, :, :, HD:HD + 1], 1.0).then_inc(made, 1)
            nc.vector.memset(KS[KS_ROWS:P, :, :], 1.0).then_inc(made, 1)
            nc.vector.memset(pv[:, :], 0.0).then_inc(made, 1)
            nc.vector.memset(MX[:], LOWEST).then_inc(made, 1)
            dve.wait_ge(made, 5)
            with dve.Fori(0, B) as b:
                for s in STEPS:
                    if s[0] == "qk":
                        n, use = qk_index[s], ring_first[s]
                        which, c = (s[2] // 2) % 2, s[2] % 2
                        wait(dve, part3, b, NQ, n - 1)
                        wait_ring_full(dve, b, use)
                        nc.vector.tensor_scalar(QF[:, n % 2, :], ring[use % 2][:, :],
                                                T["bqk"][:, 2 * which + s[1]:2 * which + s[1] + 1], None,
                                                ALU.add).then_inc(ring_free[use % 2], 1)
                        wait(dve, part1, b, NQ, n + 1)
                        nc.vector.tensor_tensor(QF[:, n % 2, :], QF[:, n % 2, :],
                                                PT[:, which, 0, c * 512:(c + 1) * 512], ALU.subtract).then_inc(rest1, 1)
                    elif s[0] == "v":
                        use = ring_first[s]
                        wait_ring_full(dve, b, use)
                        nc.vector.tensor_tensor(V1[:, s[1], :, 0:HD],
                                                ring[use % 2][:, 0:H].rearrange("p (h d) -> p h d", d=HD),
                                                T["bv"][:].rearrange("p (h d) -> p h d", d=HD),
                                                ALU.add).then_inc(ring_free[use % 2], 1)
                    elif s[0] == "scores":
                        for n, (qb, k0, k1) in enumerate(score_chunks(s[3])):
                            use = ring_first[s] + n
                            row = s[2] * TT + qb
                            wait_ring_full(dve, b, use)
                            bank = ring[use % 2]
                            if k1 < (qb + 1) * P:
                                nc.vector.tensor_reduce(MX[:, row, 2:3], bank[:, 0:512], AX.X,
                                                        ALU.max).then_inc(ring_free[use % 2], 1)
                                continue
                            w = k1 - k0 - P
                            if w:
                                nc.vector.tensor_reduce(MX[:, row, 1:2], bank[:, 0:w], AX.X, ALU.max)
                            else:
                                nc.vector.memset(tick[:, use % 2:use % 2 + 1], 0.0)
                            nc.vector.tensor_tensor_reduce(out=junk[:, use % 2, :], in0=bank[:, w:w + P], in1=causal[:], scale=1.0,
                                                           scalar=LOWEST, op0=ALU.add, op1=ALU.max,
                                                           accum_out=MX[:, row, 0:1]).then_inc(ring_free[use % 2], 1)
                    elif s[0] == "maxima":
                        last = ring_first["scores", s[1], GH - 1, 1] + 5
                        wait_ring_read(dve, b, last)
                        wait_ring_read(dve, b, last - 1)
                        nc.vector.tensor_reduce(NM[:], MX[:], AX.X, ALU.max, negate=True).then_inc(maxima_done, 1)
                    elif s[0] == "max_rows":
                        g, use = s[1], ring_first[s]
                        src = ring[use % 2][0:GH * TT, 0:P]
                        wait_ring_full(dve, b, use)
                        wait(dve, rows_ready, b, NG * 48, g * 48)
                        nc.vector.tensor_copy(MT[:, 0, :], src).then_inc(mr1, 1)
                        wait(dve, mr1, b, NG, g + 1)
                        nc.vector.tensor_tensor(MR[:], src, MT[:, 0, :], ALU.subtract).then_inc(ring_free[use % 2], 1)
                        wait_ring_read(dve, b, use)
                        nc.vector.tensor_copy(MT[:, 1, :], MR[:]).then_inc(mr2, 1)
                        wait(dve, mr2, b, NG, g + 1)
                        nc.vector.tensor_tensor(MT[:, 2, :], MR[:], MT[:, 1, :], ALU.subtract).then_inc(rows_split, 1)
                    elif s[0] == "heads_out":
                        g, half = s[1], s[2]
                        n = 2 * g + half
                        wait(dve, weights_used, b, NW, g * 12 + (4 if half == 0 else 12))
                        nc.vector.transpose(OT[:], pv[:, :]).then_inc(pv_read, 1)
                        wait(dve, pv_read, b, NO, n + 1)
                        by_token = OT[:].rearrange("p (t d) -> p t d", d=32)
                        nc.vector.reciprocal(RC[:], by_token[:, :, HD]).then_inc(o_step, 1)
                        wait(dve, o_step, b, 2 * NO, 2 * n + 1)
                        nc.vector.tensor_tensor(by_token[:, :, 0:HD], by_token[:, :, 0:HD],
                                                RC[:].unsqueeze(2).to_broadcast([P, 16, HD]), ALU.mult).then_inc(o_step, 1)
                        wait(dve, o_step, b, 2 * NO, 2 * n + 2)
                        wait(dve, packed[half], b, NG * GH * 16, g * GH * 16)
                        nc.vector.transpose(OD[:, half, :], OT[:]).then_inc(o_ready, 1)
                        wait(dve, o_ready, b, NO, n + 1)
                    elif s[0] == "up":
                        i = s[1]
                        wait(dve, squared, b, NI, i + 1)
                        nc.vector.scalar_tensor_tensor(out=A[:, i % 2, :], in0=A[:, i % 2, :], scalar=1.0,
                                                       in1=gate_b[i % 2][:, :], op0=ALU.add,
                                                       op1=ALU.mult).then_inc(cubed, 1)
                    elif s[0] == "gate":
                        i = s[1]
                        wait(dve, tanhed, b, NI, i + 1)
                        nc.vector.scalar_tensor_tensor(out=A[:, i % 2, :], in0=A[:, i % 2, :], scalar=1.0,
                                                       in1=gate_b[i % 2][:, :], op0=ALU.add,
                                                       op1=ALU.mult).then_inc(gelued, 1)
                        wait(dve, gelued, b, NI, i + 1)
                        wait(dve, up_full, b, NI, i + 1)
                        nc.vector.tensor_tensor(A[:, i % 2, :], A[:, i % 2, :], up_b[i % 2][:, :],
                                                ALU.mult).then_inc(product, 1)
                    elif s[0] == "unit":
                        u = s[1]
                        if u == 0:
                            wait(dve, bias_added, b, 1, 1)
                        wait(dve, down_done, b, NI, PAIRS * (u + 1))
                        nc.vector.tensor_tensor(res[:, 2 * u:2 * u + 2, :], acc[:, :].rearrange("p (t h) -> p t h", h=H),
                                                res[:, 2 * u:2 * u + 2, :], ALU.add).then_inc(acc_read, 1)
                    elif s[0] == "project":
                        j, use = s[1], ring_first[s]
                        if j == 0:
                            wait(dve, acc_read, b, NU, NU)
                        wait_ring_full(dve, b, use)
                        nc.vector.tensor_tensor(res[:, j, :], ring[use % 2][:, 0:H], res[:, j, :],
                                                ALU.add).then_inc(ring_free[use % 2], 1)
                        if j % 4 == 3:
                            wait_ring_read(dve, b, use)
                            wait_ring_read(dve, b, use - 1)
                            nc.vector.memset(tick[:, 2 + j // 4:3 + j // 4], 0.0).then_inc(finished, 4)

        @block.tensor
        def _(pe):
            pe.wait_ge(made, 5)

            def pair_product(dst, weights, i):
                tokens = slice((i // PAIRS) * UNIT, (i // PAIRS + 1) * UNIT)
                for nn in range(2):
                    n = 2 * (i % PAIRS) + nn
                    for k in range(KT):
                        for p, (wp, xp) in enumerate(PASSES):
                            last = nc.tensor.matmul(dst[:, nn * UNIT:(nn + 1) * UNIT], weights[:, wp, k, n * P:(n + 1) * P],
                                                    xT[:, xp, k, tokens], start=(k == 0 and p == 0),
                                                    stop=(k == KT - 1 and p == 2))
                return last

            def values(b, g, t):
                half, j, off, diagonal = weight_chunk(t)
                if j == 0:
                    wait(pe, pv_read, b, NO, 2 * g + half)
                for h in range(GH):
                    if diagonal:
                        wait(pe, masked, b, NG * len(diagonals) * GH,
                             (g * len(diagonals) + diagonals.index(t)) * GH + h + 1)
                    else:
                        wait_ring_read(pe, b, ring_first["weights", g, t] + h)
                    last = nc.tensor.matmul(pv[32 * h:32 * h + HD + 1, off:512], V1[:, j, g * GH + h, :],
                                            PR[:, (t % 2) * GH + h, 0:512 - off], start=(j == 0),
                                            stop=(t == 3 or t == 11), tile_position=(0, 32 * h))
                last.then_inc(weights_used, 1)

            with pe.Fori(0, B) as b:
                for s in STEPS:
                    if s[0] == "qk":
                        use = ring_first[s]
                        which, c = (s[2] // 2) % 2, s[2] % 2
                        col = which * H + s[1] * P
                        for u in (2 * c, 2 * c + 1):
                            wait(pe, xt_ready[u], b, 16, 16)
                        wait_ring_free(pe, b, use)
                        for k in range(KT):
                            for p, (wp, xp) in enumerate(PASSES):
                                last = nc.tensor.matmul(ring[use % 2][:, :], WA[:, wp, k, col:col + P],
                                                        xT[:, xp, k, c * 512:(c + 1) * 512],
                                                        start=(k == 0 and p == 0), stop=(k == KT - 1 and p == 2))
                        last.then_inc(ring_full[use % 2], 1)
                    elif s[0] == "v":
                        use, j = ring_first[s], s[1]
                        wait_ring_free(pe, b, use)
                        for k in range(KT):
                            for p, (wp, xp) in enumerate(PASSES):
                                last = nc.tensor.matmul(ring[use % 2][:, 0:H], xT[:, xp, k, j * P:(j + 1) * P],
                                                        WA[:, wp, k, 2 * H:3 * H],
                                                        start=(k == 0 and p == 0), stop=(k == KT - 1 and p == 2))
                        last.then_inc(ring_full[use % 2], 1)
                    elif s[0] == "scores":
                        g, h = s[1], s[2]
                        if h == 0 and s[3] == 0:
                            wait(pe, staged, b, NG * 2 * NTERM * 16, (g + 1) * 2 * NTERM * 16)
                        for n, (qb, k0, k1) in enumerate(score_chunks(s[3])):
                            use = ring_first[s] + n
                            wait_ring_free(pe, b, use)
                            nc.tensor.matmul(ring[use % 2][:, 0:k1 - k0], QS[0:KS_ROWS, h, qb * P:(qb + 1) * P],
                                             KS[0:KS_ROWS, h, k0:k1], start=True, stop=True).then_inc(ring_full[use % 2], 1)
                    elif s[0] == "max_rows":
                        g, use = s[1], ring_first[s]
                        wait(pe, maxima_done, b, NG, g + 1)
                        wait_ring_free(pe, b, use)
                        nc.tensor.transpose(ring[use % 2][0:GH * TT, 0:P], NM[:], ident[:]).then_inc(ring_full[use % 2], 1)
                    elif s[0] == "weights":
                        g, t = s[1], s[2]
                        half, j, off, diagonal = weight_chunk(t)
                        if t == 0:
                            wait(pe, rows_ready, b, NG * 48, (g + 1) * 48)
                        for h in range(GH):
                            use = ring_first[s] + h
                            wait_ring_free(pe, b, use)
                            nc.tensor.matmul(ring[use % 2][:, 0:512 - off], KS[0:KM_ROWS, h, j * P:(j + 1) * P],
                                             QS[0:KM_ROWS, h, half * 512 + off:(half + 1) * 512],
                                             start=True, stop=True).then_inc(ring_full[use % 2], 1)
                        if t:
                            values(b, g, t - 1)
                    elif s[0] == "weights_end":
                        values(b, s[1], 11)
                    elif s[0] == "up":
                        i = s[1]
                        wait(pe, product, b, NI, i - 1)
                        if i % PAIRS == 0:
                            wait(pe, xt_ready[i // PAIRS], b, 16, 16)
                        pair_product(gate_b[i % 2], WG, i).then_inc(gate_full, 1)
                        pair_product(up_b[i % 2], WU, i).then_inc(up_full, 1)
                    elif s[0] == "down":
                        i = s[1]
                        u, pair = i // PAIRS, i % PAIRS
                        if pair == 0:
                            wait(pe, acc_read, b, NU, u)
                        wait(pe, hi_done, b, NI, i + 1)
                        wait(pe, lo_done, b, NI, i + 1)
                        parts = (HI, LO)
                        for nn in range(2):
                            for tt in range(2):
                                tokens = slice(nn * UNIT + tt * P, nn * UNIT + (tt + 1) * P)
                                for p, (wp, xp) in enumerate(PASSES):
                                    last = nc.tensor.matmul(
                                        acc[:, tt * H:(tt + 1) * H], parts[xp][:, i % 2, tokens], WD[:, wp, 2 * pair + nn, :],
                                        start=(pair == 0 and nn == 0 and tt == 0 and p == 0),
                                        stop=(pair == PAIRS - 1 and nn == 1 and p == 2), skip_group_check=True)
                        last.then_inc(down_done, 1)
                    elif s[0] == "project":
                        j, use = s[1], ring_first[s]
                        if j == 0:
                            for half in range(2):
                                wait(pe, packed[half], b, NG * GH * 16, NG * GH * 16)
                        wait_ring_free(pe, b, use)
                        for k in range(KT):
                            last = nc.tensor.matmul(ring[use % 2][:, 0:H], OP[:, k, j * P:(j + 1) * P], WP[:, k, :],
                                                    start=(k == 0), stop=(k == KT - 1))
                        last.then_inc(ring_full[use % 2], 1)


_INS = ["L0_attn_encodings", "L0_attn_w_attn", "L0_attn_b_attn", "L0_attn_w_proj", "L0_attn_b_proj",
        "L0_ffn_gate_W_packed", "L0_ffn_gate_scales", "L0_ffn_up_W_packed", "L0_ffn_up_scales",
        "L0_ffn_down_W_packed", "L0_ffn_down_scales"]


def kernel(**inputs):
    import numpy as _np
    import concourse.bacc as _bacc
    from concourse import mybir as _mybir
    from concourse.bass_utils import run_bass_kernel_spmd as _run

    nc = _bacc.Bacc("TRN2", target_bir_lowering=False, num_devices=1, dynamic_dma_scratch_size=1024)
    arrays, args = {}, []
    for name in _INS:
        a = _np.ascontiguousarray(inputs[name])
        arrays[f"in_{name}"] = a
        args.append(nc.dram_tensor(f"in_{name}", a.shape, _mybir.dt.from_np(a.dtype), kind="ExternalInput").ap())
    args.append(nc.dram_tensor("out_0", (B, S, H), _mybir.dt.float32, kind="ExternalOutput").ap())
    build(nc, *args)
    r = _run(nc, [arrays], core_ids=[0])
    return r.results[0]["out_0"]
```

```python
import concourse.bass as bass
from concourse import mybir
from contextlib import ExitStack

f32 = mybir.dt.float32
f32r = mybir.dt.float32r
bf16 = mybir.dt.bfloat16
i32 = mybir.dt.int32
fp8 = mybir.dt.float8e4
ALU = mybir.AluOpType
ACT = mybir.ActivationFunctionType
AX = mybir.AxisListType

P = 128
B, S, H = 4, 1024, 256
NH, HD = 16, 16
F = 2048
KT = H // P
NT = F // P
TT = S // P
UNIT = 256
NU = S // UNIT
PAIRS = NT // 2
NI = NU * PAIRS
GH = 4
NG = NH // GH
BLK = 32
RUNS_Q = ((0, 3, 0, True), (3, 2, 0, True), (5, 1, 0, True))
RUNS_K = ((0, 3, 0, False), (3, 2, 1, False), (5, 1, 2, False))
NTERM = 6
KS_ROWS = NTERM * HD
KM_ROWS = KS_ROWS + 3
LOWEST = -3.0e38
EPS = 1e-5
PASSES = ((0, 0), (0, 1), (1, 0))


def ffn_pieces():
    pieces = [[] for _ in range(PIECES)]
    for i in range(NI):
        for n, step in ((0, ("gate", i, 0)), (1, ("gate", i, 1)), (2, ("up", i, 0)), (3, ("up", i, 1)),
                        (2, ("square", i)), (3, ("cube", i)), (4, ("tanh", i)), (5, ("gelu", i)),
                        (6, ("times_up", i)), (7, ("high", i)), (8, ("low", i)),
                        (10, ("down", i, 0)), (11, ("down", i, 1))):
            pieces[6 * i + n].append(step)
        if i % PAIRS == PAIRS - 1:
            pieces[6 * i + 12].append(("unit", i // PAIRS))
    return pieces


def sequence_steps():
    pieces = ffn_pieces()[::-1]
    steps = []

    def with_ffn(count, own):
        done = 0
        for n, step in enumerate(own):
            steps.extend(step)
            while done < count * (n + 1) // len(own):
                steps.extend(pieces.pop())
                done += 1

    def scores(g):
        return [("scores", g, h, n) for h in range(GH) for n in range(len(CHUNKS))]

    products = [("qk", n) for n in range(4)] + [("v", j) for j in range(TT)] + [("qk", n) for n in range(4, 8)]
    own = [[p] for p in products]
    for n, p in enumerate(products):
        if p[0] == "qk":
            own[min(n + 1, len(own) - 1)].append(("qk_parts", p[1]))
    own[5] += [("stage", 0), ("stage", 1)]
    with_ffn(PIECES_QKV, own)
    with_ffn(PIECES_SCORES, [[s] for s in scores(0)])
    with_ffn(PIECES_MAXIMA, [[("maxima", 0)], [], [], [("max_rows", 0)], [], [], []])
    for g in range(NG):
        own = [[("weights", g, t, h)] for t in range(WSTEPS) for h in range(GH)]
        if g:
            own[GH - 1].append(("values", g - 1, WSTEPS - 1))
            own[GH + 1].append(("heads_out", g - 1, 1))
        for t in range(1, WSTEPS):
            own[t * GH + GH - 1].append(("values", g, t - 1))
        own[5 * GH + 1].append(("heads_out", g, 0))
        if g < NG - 1:
            first, last = (0, 36) if g == 0 else (8, 39)
            for n, s in enumerate(scores(g + 1)):
                own[first + n * (last - first) // (GH * len(CHUNKS))].append(s)
            own[last].append(("maxima", g + 1))
            own[last + 2].append(("max_rows", g + 1))
            own[-1].append(("stage", g + 2) if g < NG - 2 else ("fetch", 0))
        with_ffn(PIECES_GROUP if g < NG - 1 else PIECES_LAST, own)
    steps += [("values", NG - 1, WSTEPS - 1)]
    with_ffn(2, [[], []])
    steps += [("heads_out", NG - 1, 1), ("fetch", 1)]
    while pieces:
        steps.extend(pieces.pop())
    steps += [("project", j) for j in range(TT)]
    return steps


PIECES = 6 * NI + 7
PIECES_QKV = 16
PIECES_SCORES = 30
PIECES_MAXIMA = 8
PIECES_GROUP = 36
PIECES_LAST = 20

CHUNKS = [(qb, k0, min(k0 + 512, (qb + 1) * P)) for qb in range(TT) for k0 in range(0, (qb + 1) * P, 512)]
WSTEPS = 12


def weight_step(t):
    half, j = (0, t) if t < 4 else (1, t - 4)
    diagonal = j >= 4 * half
    return half, j, P * (j - 4 * half) if diagonal else 0, diagonal


def build(nc, x_in, w_attn, b_attn, w_proj, b_proj, gate_w, gate_s, up_w, up_s, down_w, down_s, out):
    STEPS = sequence_steps()

    vring = {u: n for n, u in enumerate(u for u in STEPS if u[0] in ("qk", "v", "scores", "max_rows", "project"))}
    wring = {u: n for n, u in enumerate(u for u in STEPS if u[0] == "weights")}
    assert len(vring) % 2 == 0 and len(wring) % 2 == 0

    top = ExitStack()
    with top:
        def sb(name, shape, dt, where=None):
            return (where or top).enter_context(nc.sbuf_tensor(name, shape, dt))

        def sem(name, where=None):
            return (where or top).enter_context(nc.semaphore(name))

        WG = sb("WG", [P, 2, KT, F], f32r)
        WU = sb("WU", [P, 2, KT, F], f32r)
        WD = sb("WD", [P, 2, NT, H], f32r)
        WA = sb("WA", [P, 2, KT, 3 * H], f32r)
        WP = sb("WP", [P, KT, H], f32)
        bqk = sb("bqk", [P, 4], f32)
        bv = sb("bv", [P, H], f32)
        bp = sb("bp", [P, H], f32)
        ident = sb("ident", [P, P], f32)
        causal = sb("causal", [P, P], bf16)
        bqk_dram = nc.dram_tensor("bqk_by_dim", (4, P), f32, kind="Internal").ap()
        banks = [top.enter_context(nc.psum_tensor(f"bank{i}", [P, 512], f32)) for i in range(8)]
        qk_dram = nc.dram_tensor("qk_parts", (2, 2, NTERM, P, S), bf16, kind="Internal").ap()
        o_dram = nc.dram_tensor("head_outputs", (NG, P, S), f32, kind="Internal").ap()
        xn_dram = nc.dram_tensor("xn_parts", (B, NU, P, 2, KT, UNIT), f32, kind="Internal").ap()

        setup_phase(nc, sem, sb, banks, locals())
        main_phase(nc, sem, sb, banks, locals(), STEPS, vring, wring)


def setup_phase(nc, sem, sb, banks, T):
    WG, WU, WD, WA, WP = T["WG"], T["WU"], T["WD"], T["WA"], T["WP"]
    ident, causal, xn_dram = T["ident"], T["causal"], T["xn_dram"]
    NX = B * S // P
    NC = 12
    CW = 512
    with ExitStack() as own:
        X = sb("X", [P, NX, H], f32, own)
        stats = sb("stats", [P, NX, 6], f32, own)
        mv = sb("mv", [P, NX, 2], f32, own)
        rs = sb("rs", [P, 4, NX], f32, own)
        XS = sb("XS", [P, 2, 2, KT, 512], f32r, own)
        PK = sb("PK", [P, 2, CW], i32, own)
        CODE = sb("CODE", [P, 4, CW], i32, own)
        WF = sb("WF", [P, 2, 2 * CW], f32, own)
        SC = sb("SC", [P, 3, P], f32, own)
        WT = sb("WT", [P, KT, 3 * H], f32, own)

        x_loaded = [sem(f"x_loaded{b}", own) for b in range(B)]
        wa_loaded, wp_loaded, bias_loaded, sc_loaded = (sem(n, own) for n in ("wa_loaded", "wp_loaded", "bias_loaded", "sc_loaded"))
        bias_ordered = sem("bias_ordered", own)
        pk_loaded = [sem(f"pk_loaded{i}", own) for i in range(2)]
        consts_made = sem("consts_made", own)
        dve_step = sem("dve_step", own)
        var_ready, root_ready, xn_ready = (sem(n, own) for n in ("var_ready", "root_ready", "xn_ready"))
        xt_full, x_hi, x_lo = (sem(n, own) for n in ("xt_full", "x_hi", "x_lo"))
        xs_stored = [sem(f"xs_stored{i}", own) for i in range(2)]
        wa_hi, code_read, wf_ready, wt_full, w_hi, w_lo = (sem(n, own) for n in ("wa_hi", "code_read", "wf_ready", "wt_full", "w_hi", "w_lo"))
        block = own.enter_context(nc.Block())

        def packed(c):
            if c < 8:
                w = T["gate_w"] if c < 4 else T["up_w"]
                return w[(c % 4) * 512:(c % 4 + 1) * 512, :].rearrange("(i p) w -> p i w", p=P)
            c -= 8
            return T["down_w"][(c // 2) * P:(c // 2 + 1) * P, (c % 2) * CW:(c % 2 + 1) * CW]

        def attn_columns():
            for m in range(4):
                cols = slice(m * P, (m + 1) * P)
                yield WT[:, :, cols].rearrange("p k (h r) -> p k r h", h=8), cols
            yield WT[:, :, 2 * H:3 * H], slice(2 * H, 3 * H)

        def weight_dest(c, part, k):
            if c < 8:
                return (WG if c < 4 else WU)[:, part, k, (c % 4) * 512:(c % 4 + 1) * 512]
            c -= 8
            nt = (c % 2) * 8 + 4 * k
            return WD[:, part, nt:nt + 4, (c // 2) * P:(c // 2 + 1) * P]

        def bank_view(bank, c):
            return bank[:, :] if c < 8 else bank[:, :].rearrange("p (n h) -> p n h", h=P)

        @block.sync
        def _(sp):
            for b in range(B):
                sp.dma_start(X[:, b * TT:(b + 1) * TT, :],
                             T["x_in"][b].rearrange("(t p) h -> p t h", p=P)).then_inc(x_loaded[b], 16)
                if b == 0:
                    sp.dma_start(SC[:, 0, :].rearrange("p (t s) -> p t s", s=8),
                                 T["gate_s"].rearrange("(t p) s -> p t s", p=P)).then_inc(sc_loaded, 16)
                    sp.dma_start(SC[:, 1, :].rearrange("p (t s) -> p t s", s=8),
                                 T["up_s"].rearrange("(t p) s -> p t s", p=P)).then_inc(sc_loaded, 16)
                    sp.dma_start(SC[:, 2, :].rearrange("p (t s) -> p t s", s=64),
                                 T["down_s"].rearrange("(t p) s -> p t s", p=P)).then_inc(sc_loaded, 16)
                    sp.dma_start(WT[:], T["w_attn"].rearrange("(k p) n -> p k n", p=P)).then_inc(wa_loaded, 16)
                    sp.dma_start(WP[:], T["w_proj"].rearrange("(k p) n -> p k n", p=P)).then_inc(wp_loaded, 16)
                    for i in range(2):
                        sp.dma_start(PK[:, i, :].rearrange("p (i w) -> p i w", w=P), packed(i)).then_inc(pk_loaded[i], 16)
                    for m in range(4):
                        sp.dma_start(T["bqk_dram"][m].rearrange("(r h) -> r h", h=8),
                                     T["b_attn"][m * P:(m + 1) * P].rearrange("(h r) -> r h", h=8),
                                     allow_slow_non_contiguous=True).then_inc(bias_ordered, 16)
                    sp.dma_start(T["bv"][:], T["b_attn"][2 * H:3 * H].partition_broadcast(P)).then_inc(bias_loaded, 16)
                    sp.dma_start(T["bp"][:], T["b_proj"].partition_broadcast(P)).then_inc(bias_loaded, 16)
            for c in range(B * S // 512):
                sp.wait_ge(x_lo, 2 * c + 2)
                for u in range(2):
                    sp.dma_start(xn_dram[c // 2, 2 * (c % 2) + u],
                                 XS[:, c % 2, :, :, u * UNIT:(u + 1) * UNIT].bitcast(f32)).then_inc(xs_stored[c % 2], 16)
            for c in range(2, NC):
                sp.wait_ge(code_read, c - 1)
                dst = PK[:, c % 2, :]
                if c < 8:
                    dst = dst.rearrange("p (i w) -> p i w", w=P)
                sp.dma_start(dst, packed(c)).then_inc(pk_loaded[c % 2], 16)
            sp.wait_ge(bias_ordered, 64)
            sp.dma_start(T["bqk"][:], T["bqk_dram"].rearrange("t p -> p t"),
                         allow_slow_non_contiguous=True).then_inc(bias_loaded, 16)
            for i in range(2):
                sp.wait_ge(xs_stored[i], 16 * B * S // 512)
            sp.wait_ge(wp_loaded, 16)
            sp.wait_ge(bias_loaded, 48)

        @block.gpsimd
        def _(pool):
            nc.gpsimd.memset(ident[:], 0.0).then_inc(consts_made, 1)
            nc.gpsimd.memset(causal[:], 0.0).then_inc(consts_made, 1)
            pool.wait_ge(consts_made, 2)
            nc.gpsimd.affine_select(out=ident[:], in_=ident[:], compare_op=ALU.not_equal, fill=1.0, base=0,
                                    pattern=[[-1, P]], channel_multiplier=1).then_inc(consts_made, 1)
            nc.gpsimd.affine_select(out=causal[:], in_=causal[:], compare_op=ALU.is_ge, fill=LOWEST, base=0,
                                    pattern=[[-1, P]], channel_multiplier=1).then_inc(consts_made, 1)

        @block.vector
        def _(dve):
            done = [0]

            def link(ins):
                ins.then_inc(dve_step, 1)
                done[0] += 1
                dve.wait_ge(dve_step, done[0])

            def lo_parts(c):
                for k in range(KT):
                    dve.wait_ge(x_hi, 2 * c + k + 1)
                    if c >= 2:
                        dve.wait_ge(xs_stored[c % 2], 32 * (c // 2))
                    nc.vector.tensor_tensor(XS[:, c % 2, 1, k, :], banks[4 + 2 * (c % 2) + k][:, :],
                                            XS[:, c % 2, 0, k, :].bitcast(f32), ALU.subtract).then_inc(x_lo, 1)

            for b in range(B):
                dve.wait_ge(x_loaded[b], 16)
                own_tiles = slice(b * TT, (b + 1) * TT)
                for t in range(b * TT, (b + 1) * TT):
                    last = nc.vector.bn_stats(stats[:, t, :], X[:, t, :])
                link(last)
                for t in range(b * TT, (b + 1) * TT):
                    last = nc.vector.bn_aggr(mv[:, t, :], stats[:, t, :])
                link(last)
                nc.vector.tensor_scalar(rs[:, 0, own_tiles], mv[:, own_tiles, 1], EPS, None,
                                        ALU.add).then_inc(var_ready, 1)
                dve.wait_ge(var_ready, b + 1)
                dve.wait_ge(root_ready, b + 1)
                link(nc.vector.reciprocal(rs[:, 2, own_tiles], rs[:, 1, own_tiles]))
                link(nc.vector.tensor_tensor(rs[:, 3, own_tiles], rs[:, 2, own_tiles], rs[:, 2, own_tiles], ALU.mult))
                link(nc.vector.tensor_tensor(rs[:, 3, own_tiles], rs[:, 3, own_tiles], rs[:, 0, own_tiles], ALU.mult))
                link(nc.vector.tensor_scalar(rs[:, 3, own_tiles], rs[:, 3, own_tiles], -0.5, 1.5, ALU.mult, ALU.add))
                link(nc.vector.tensor_tensor(rs[:, 2, own_tiles], rs[:, 2, own_tiles], rs[:, 3, own_tiles], ALU.mult))
                for t in range(b * TT, (b + 1) * TT):
                    nc.vector.tensor_scalar(X[:, t, :], X[:, t, :], mv[:, t, 0:1], rs[:, 2, t:t + 1],
                                            ALU.subtract, ALU.mult).then_inc(xn_ready, 1)
                for c in (2 * b, 2 * b + 1):
                    lo_parts(c)
            dve.wait_ge(wa_hi, 5)
            for src, dst in attn_columns():
                which_hi = WA[:, 0, :, dst].bitcast(f32)
                nc.vector.tensor_tensor(WA[:, 1, :, dst], src, which_hi, ALU.subtract)
            dve.wait_ge(sc_loaded, 48)
            nc.vector.tensor_scalar(SC[:, 0:2], SC[:, 0:2], 64.0, None, ALU.mult)
            link(nc.vector.tensor_scalar(SC[:, 2], SC[:, 2], 32.0, None, ALU.mult))

            def w_lo_parts(c):
                for k in range(2):
                    dve.wait_ge(w_hi, 2 * c + k + 1)
                    nc.vector.tensor_tensor(weight_dest(c, 1, k), bank_view(banks[2 * (c % 2) + k], c),
                                            weight_dest(c, 0, k).bitcast(f32), ALU.subtract).then_inc(w_lo, 1)

            for c in range(NC):
                dve.wait_ge(pk_loaded[c % 2], 16 * (c // 2 + 1))
                src = PK[:, c % 2, :]
                for i, (shift, mask) in enumerate(((2, 0x1C), (4, 0x80), (6, 0x1C00), (8, 0x8000))):
                    last = nc.vector.tensor_scalar(CODE[:, i, :], src, shift, mask, ALU.logical_shift_left, ALU.bitwise_and)
                last.then_inc(code_read, 1)
                dve.wait_ge(code_read, c + 1)
                link(nc.vector.tensor_tensor(CODE[:, 0:2, :], CODE[:, 0:2, :], CODE[:, 2:4, :], ALU.bitwise_or))
                link(nc.vector.tensor_tensor(CODE[:, 0, :], CODE[:, 0, :], CODE[:, 1, :], ALU.bitwise_or))
                if c >= 2:
                    dve.wait_ge(wt_full, 2 * c - 2)
                which, first = (c // 4, (c % 4) * 32) if c < 8 else (2, ((c - 8) // 2) * 64 + (c % 2) * 32)
                scale = SC[:, which, first:first + 32].unsqueeze(2).unsqueeze(3).to_broadcast([P, 32, BLK // 2, 2])
                code = CODE[:, 0, :].bitcast(fp8).rearrange("p (b w c) -> p b w c", b=32, c=4)[:, :, :, 0:2]
                nc.vector.tensor_tensor(WF[:, c % 2, :].rearrange("p (b w c) -> p b w c", b=32, c=2),
                                        code, scale, ALU.mult).then_inc(wf_ready, 1)
                dve.wait_ge(wf_ready, c + 1)
                if c:
                    w_lo_parts(c - 1)
            w_lo_parts(NC - 1)

        @block.scalar
        def _(act):
            def hi_parts(c):
                for k in range(KT):
                    act.wait_ge(xt_full, 2 * c + k + 1)
                    if c >= 2:
                        act.wait_ge(xs_stored[c % 2], 32 * (c // 2))
                    nc.scalar.activation(XS[:, c % 2, 0, k, :], banks[4 + 2 * (c % 2) + k][:, :],
                                         ACT.Copy).then_inc(x_hi, 1)

            for b in range(B):
                act.wait_ge(var_ready, b + 1)
                own_tiles = slice(b * TT, (b + 1) * TT)
                nc.scalar.activation(rs[:, 1, own_tiles], rs[:, 0, own_tiles], ACT.Sqrt).then_inc(root_ready, 1)
                for c in (2 * b, 2 * b + 1):
                    hi_parts(c)
            act.wait_ge(wa_loaded, 16)
            for src, dst in attn_columns():
                nc.scalar.activation(WA[:, 0, :, dst], src, ACT.Copy).then_inc(wa_hi, 1)
            for c in range(NC):
                for k in range(2):
                    act.wait_ge(wt_full, 2 * c + k + 1)
                    nc.scalar.activation(weight_dest(c, 0, k), bank_view(banks[2 * (c % 2) + k], c),
                                         ACT.Copy).then_inc(w_hi, 1)

        @block.tensor
        def _(pe):
            pe.wait_ge(consts_made, 4)
            for c in range(B * S // 512):
                for k in range(KT):
                    if c >= 2:
                        pe.wait_ge(x_lo, 2 * (c - 2) + k + 1)
                    for i in range(4):
                        t = 4 * c + i
                        pe.wait_ge(xn_ready, t + 1)
                        last = nc.tensor.transpose(banks[4 + 2 * (c % 2) + k][:, i * P:(i + 1) * P],
                                                   X[:, t, k * P:(k + 1) * P], ident[:])
                    last.then_inc(xt_full, 1)
            for c in range(NC):
                pe.wait_ge(wf_ready, c + 1)
                for k in range(2):
                    if c >= 2:
                        pe.wait_ge(w_lo, 2 * (c - 2) + k + 1)
                    for i in range(4):
                        col = (i * KT + k) * P if c < 8 else (4 * k + i) * P
                        last = nc.tensor.transpose(banks[2 * (c % 2) + k][:, i * P:(i + 1) * P],
                                                   WF[:, c % 2, col:col + P], ident[:])
                    last.then_inc(wt_full, 1)


def main_phase(nc, sem, sb, banks, T, STEPS, vring, wring):
    WG, WU, WD, WA, WP = T["WG"], T["WU"], T["WD"], T["WA"], T["WP"]
    ident, causal, xn_dram, qk_dram, o_dram = T["ident"], T["causal"], T["xn_dram"], T["qk_dram"], T["o_dram"]
    acc, gate_b, up_b, pv = banks[0], banks[1], banks[2], banks[3]
    vbank, wbank = banks[4:6], banks[6:8]
    with ExitStack() as own:
        xT = sb("xT", [P, 2, KT, S], f32r, own)
        res = sb("res", [P, TT, H], f32, own)
        QF = sb("QF", [P, 2, 512], f32, own)
        PT = sb("PT", [P, 2, 3, 512], bf16, own)
        QS = sb("QS", [P, 2, GH, S], bf16, own)
        KS = sb("KS", [P, 2, GH, S], bf16, own)
        V1 = sb("V1", [P, TT, NH, HD + 1], f32, own)
        junk = sb("junk", [P, 2, P], bf16, own)
        tick = sb("tick", [P, 4], f32, own)
        carry = sb("carry", [1, WSTEPS + 1], f32, own)
        carried = sb("carried", [1, 8], f32, own)
        MX = sb("MX", [P, GH * TT, 3], f32, own)
        NM = sb("NM", [P, GH * TT], f32, own)
        MR = sb("MR", [GH * TT, P], f32, own)
        MT = sb("MT", [GH * TT, 3, P], bf16, own)
        PR = sb("PR", [P, 2, GH, 512], f32, own)
        OT = sb("OT", [P, 512], f32, own)
        RC = sb("RC", [P, 16], f32, own)
        OD = sb("OD", [P, 512], f32, own)
        A = sb("A", [P, 2, 512], f32, own)
        G = sb("G", [P, 512], f32, own)
        U = sb("U", [P, 512], f32, own)
        HI = sb("HI", [P, 512], f32r, own)
        LO = sb("LO", [P, 512], f32r, own)
        OP = QS[:, 0].rearrange("p h t -> p (h t)").bitcast(f32).rearrange("p (k t) -> p k t", k=KT)

        made = sem("made", own)
        xt_ready = [sem(f"xt_ready{u}", own) for u in range(NU)]
        x_ready, bias_added = sem("x_ready", own), sem("bias_added", own)
        v_full, v_free, w_full, w_free = (sem(n, own) for n in ("v_full", "v_free", "w_full", "w_free"))
        part1, rest1, part2, part3 = (sem(n, own) for n in ("part1", "rest1", "part2", "part3"))
        spilled = [sem(f"spilled{m}", own) for m in range(2)]
        staged = [[sem(f"staged{m}_{h}", own) for h in range(2)] for m in range(2)]
        maxima_done, mr1, mr2, rows_split, rows_ready = (
            sem(n, own) for n in ("maxima_done", "mr1", "mr2", "rows_split", "rows_ready"))
        masked, values_done = sem("masked", own), sem("values_done", own)
        pv_read, o_step, o_ready, o_stored, packed = (
            sem(n, own) for n in ("pv_read", "o_step", "o_ready", "o_stored", "packed"))
        gate_full, up_full, gate_copied, squared, cubed, tanhed, up_copied, gelued, product, hi_done, lo_done = (
            sem(n, own) for n in ("gate_full", "up_full", "gate_copied", "squared", "cubed", "tanhed", "up_copied",
                                  "gelued", "product", "hi_done", "lo_done"))
        down_done, acc_read = sem("down_done", own), sem("acc_read", own)
        carried_out, finished, stored = sem("carried_out", own), sem("finished", own), sem("stored", own)
        counted = [x_ready, bias_added, v_full, v_free, w_full, w_free, part1, rest1, part2, part3, maxima_done, mr1,
                   mr2, rows_split, rows_ready, masked, values_done, pv_read, o_step, o_ready, o_stored, packed,
                   gate_full, up_full, gate_copied, squared, cubed, tanhed, up_copied, gelued, product, hi_done,
                   lo_done, down_done, acc_read, finished, stored, *xt_ready, *spilled, *staged[0], *staged[1]]
        block = own.enter_context(nc.Block())

        NQ, NW, NO = 8, NG * WSTEPS, NG * 2
        NV, NWR = len(vring), len(wring)
        diagonals = [t for t in range(WSTEPS) if weight_step(t)[3]]
        ND = NG * len(diagonals)
        SPILL = 3 * 16

        def wait(eng, s, b, per, k):
            eng.wait_ge(s, b * per + (max(k, 0) + 1))

        def qk_chunk(n):
            return n // 4, (n // 2) % 2, n % 2

        @block.sync
        def _(sp):
            for s in counted:
                sp.sem_inc(s, 1)
            sp.wait_ge(made, 5)

            def carrier(n):
                sp.dma_start(carried[:, n:n + 1], tick[0:1, 0:1]).then_inc(carried_out, 16)

            with sp.Fori(0, B) as b:
                for s in STEPS:
                    if s[0] == "qk_parts":
                        n = s[1]
                        m, which, c = qk_chunk(n)
                        wait(sp, part3, b, NQ, n + 1)
                        for first, count, part, changes in (RUNS_Q, RUNS_K)[which]:
                            src = (PT[:, n % 2, part:part + count, :] if changes else
                                   PT[:, n % 2, part:part + 1, :].to_broadcast([P, count, 512]))
                            dst = qk_dram[m, which, first:first + count, :, c * 512:(c + 1) * 512]
                            sp.dma_start(dst.rearrange("c p t -> p c t"), src).then_inc(spilled[n % 2], 16)
                    elif s[0] == "stage":
                        g = s[1]
                        m, first = g // 2, (g % 2) * GH
                        if g % 2 == 0:
                            wait(sp, spilled[0], b, 4 * SPILL, 2 * SPILL * (m + 1))
                            carrier(0)
                            wait(sp, spilled[1], b, 4 * SPILL, 2 * SPILL * (m + 1))
                            carrier(1)
                        if g > 1:
                            wait(sp, w_full, b, NWR, wring["weights", g - 2, WSTEPS - 1, GH - 1] + 1)
                        for h in (0, 2):
                            for which, dst in ((1, KS), (0, QS)):
                                src = qk_dram[m, which].rearrange("c (r h) t -> (c r) h t", h=8)
                                sp.dma_start(dst[0:KS_ROWS, g % 2, h:h + 2],
                                             src[:, first + h:first + h + 2]).then_inc(staged[g % 2][h // 2], 16)
                    elif s[0] == "max_rows":
                        g = s[1]
                        wait(sp, rows_split, b, NG, g + 1)
                        for c in range(3):
                            sp.dma_start(QS[KS_ROWS + c:KS_ROWS + c + 1, g % 2].rearrange("o h (q t) -> o (h q) t", t=P),
                                         MT[:, c, :]).then_inc(rows_ready, 16)
                    elif s[0] == "heads_out":
                        g, half = s[1], s[2]
                        wait(sp, o_ready, b, NO, 2 * g + half + 1)
                        sp.dma_start(o_dram[g, :, half * 512:(half + 1) * 512], OD[:]).then_inc(o_stored, 16)
                    elif s[0] == "fetch":
                        groups = range(NG - 1) if s[1] == 0 else [NG - 1]
                        wait(sp, o_stored, b, NO * 16, 32 * groups[-1] + (16 if s[1] == 0 else 32))
                        if s[1] == 0:
                            carrier(4)
                            wait(sp, w_full, b, NWR, wring["weights", NG - 2, WSTEPS - 1, GH - 1] + 1)
                        for g in groups:
                            if s[1] == 0 and g == NG - 2:
                                continue
                            for h in range(GH):
                                row = ((g % 2) * GH + h) * HD
                                sp.dma_start(OP[row:row + HD, g // 2, :],
                                             o_dram[g, 32 * h:32 * h + HD, :]).then_inc(packed, 16)
                        if s[1] == 1:
                            for h in range(GH):
                                row = h * HD
                                sp.dma_start(OP[row:row + HD, 1, :],
                                             o_dram[NG - 2, 32 * h:32 * h + HD, :]).then_inc(packed, 16)
                    elif s[0] == "project" and s[1] % 4 == 3:
                        j = s[1] - 3
                        wait(sp, finished, b, TT, j + 4)
                        carrier(2 + j // 4)
                        sp.dma_start(T["out"][b].rearrange("(t p) h -> p t h", p=P)[:, j:j + 4, :],
                                     res[:, j:j + 4, :]).then_inc(stored, 16)
            sp.wait_ge(stored, B * 32 + 1)
            sp.wait_ge(carried_out, B * 7 * 16)

        @block.gpsimd
        def _(pool):
            nc.gpsimd.memset(carry[:], 0.0).then_inc(made, 1)
            pool.wait_ge(made, 5)

            def carrier(n):
                nc.gpsimd.tensor_tensor(carry[:, n:n + 1], carry[:, WSTEPS:], carry[:, WSTEPS:], ALU.add)

            with pool.Fori(0, B) as b:
                for s in STEPS:
                    if s[0] == "qk_parts":
                        n = s[1]
                        wait(pool, part2, b, NQ, n + 1)
                        nc.gpsimd.tensor_tensor(PT[:, n % 2, 2, :], QF[:, n % 2], PT[:, n % 2, 1, :],
                                                ALU.subtract).then_inc(part3, 1)
                    elif s == ("v", TT - 1):
                        wait(pool, x_ready, b, 16, 16)
                        nc.gpsimd.tensor_tensor(res[:], res[:], T["bp"][:].unsqueeze(1).to_broadcast([P, TT, H]),
                                                ALU.add).then_inc(bias_added, 1)
                    elif s[0] == "values":
                        g, t = s[1:]
                        half, j, off, diagonal = weight_step(t)
                        if diagonal:
                            wait(pool, w_free, b, NWR, wring["weights", g, t, GH - 1] + 1)
                            carrier(t)
                            block_ = PR[:, t % 2, :, 0:P]
                            nc.gpsimd.affine_select(out=block_, in_=block_, compare_op=ALU.is_ge, fill=0.0, base=0,
                                                    pattern=[[0, GH], [1, P]], channel_multiplier=-1).then_inc(masked, 1)
                    elif s[0] == "times_up":
                        i = s[1]
                        wait(pool, gelued, b, NI, i + 1)
                        wait(pool, up_copied, b, NI, i + 1)
                        nc.gpsimd.tensor_tensor(A[:, i % 2, :], A[:, i % 2, :], U[:], ALU.mult).then_inc(product, 1)
                    elif s[0] == "low":
                        i = s[1]
                        wait(pool, hi_done, b, NI, i + 1)
                        nc.gpsimd.tensor_tensor(LO[:], A[:, i % 2, :], HI[:].bitcast(f32),
                                                ALU.subtract).then_inc(lo_done, 1)

        @block.scalar
        def _(act):
            act.wait_ge(made, 5)
            with act.Fori(0, B) as b:
                wait(act, up_full, b, NI, 0)
                for u in range(NU):
                    act.dma_start(xT[:, :, :, u * UNIT:(u + 1) * UNIT].bitcast(f32), xn_dram[b, u]).then_inc(xt_ready[u], 16)
                for s in STEPS:
                    if s[0] == "qk_parts":
                        n, use = s[1], vring["qk", s[1]]
                        wait(act, v_free, b, NV, use + 1)
                        wait(act, spilled[n % 2], b, 4 * SPILL, SPILL * (n // 2))
                        nc.scalar.activation(PT[:, n % 2, 0, :], QF[:, n % 2], ACT.Copy).then_inc(part1, 1)
                        wait(act, rest1, b, NQ, n + 1)
                        nc.scalar.activation(PT[:, n % 2, 1, :], QF[:, n % 2], ACT.Copy).then_inc(part2, 1)
                    elif s == ("v", TT - 1):
                        wait(act, stored, b, 32, 0)
                        act.dma_start(res[:], T["x_in"][b].rearrange("(t p) h -> p t h", p=P)).then_inc(x_ready, 16)
                    elif s[0] == "weights":
                        g, t, h = s[1:]
                        use = wring[s]
                        half, j, off, diagonal = weight_step(t)
                        if h == 0:
                            wait(act, values_done, b, NW, g * WSTEPS + t - 1)
                        wait(act, w_full, b, NWR, use + 1)
                        nc.scalar.activation(PR[:, t % 2, h, 0:512 - off], wbank[use % 2][:, 0:512 - off],
                                             ACT.Exp, scale=0.25).then_inc(w_free, 1)
                    elif s[0] == "square":
                        i = s[1]
                        wait(act, gate_full, b, NI, i + 1)
                        wait(act, gelued, b, NI, i)
                        nc.scalar.activation(G[:], gate_b[:, :], ACT.Copy).then_inc(gate_copied, 1)
                        wait(act, lo_done, b, NI, i - 1)
                        nc.scalar.activation(A[:, i % 2, :], gate_b[:, :], ACT.Square,
                                             scale=0.044715 ** 0.5).then_inc(squared, 1)
                    elif s[0] == "tanh":
                        i = s[1]
                        wait(act, up_full, b, NI, i + 1)
                        wait(act, product, b, NI, i)
                        nc.scalar.activation(U[:], up_b[:, :], ACT.Copy).then_inc(up_copied, 1)
                        wait(act, cubed, b, NI, i + 1)
                        nc.scalar.activation(A[:, i % 2, :], A[:, i % 2, :], ACT.Tanh,
                                             scale=0.7978845608028654).then_inc(tanhed, 1)
                    elif s[0] == "high":
                        i = s[1]
                        wait(act, product, b, NI, i + 1)
                        wait(act, down_done, b, NI, i)
                        nc.scalar.activation(HI[:], A[:, i % 2, :], ACT.Copy).then_inc(hi_done, 1)

        @block.vector
        def _(dve):
            nc.vector.memset(V1[:, :, :, HD:HD + 1], 1.0).then_inc(made, 1)
            nc.vector.memset(KS[KS_ROWS:P, :, :, :], 1.0).then_inc(made, 1)
            nc.vector.memset(pv[:, :], 0.0).then_inc(made, 1)
            nc.vector.memset(tick[:], 0.0)
            nc.vector.memset(MX[:], LOWEST).then_inc(made, 1)
            dve.wait_ge(made, 5)
            with dve.Fori(0, B) as b:
                for s in STEPS:
                    if s[0] == "qk":
                        n, use = s[1], vring[s]
                        m, which, c = qk_chunk(n)
                        wait(dve, part3, b, NQ, n - 1)
                        wait(dve, v_full, b, NV, use + 1)
                        nc.vector.tensor_scalar(QF[:, n % 2], vbank[use % 2][:, :],
                                                T["bqk"][:, 2 * which + m:2 * which + m + 1],
                                                None, ALU.add).then_inc(v_free, 1)
                    elif s[0] == "qk_parts":
                        n = s[1]
                        wait(dve, part1, b, NQ, n + 1)
                        nc.vector.tensor_tensor(QF[:, n % 2], QF[:, n % 2], PT[:, n % 2, 0, :],
                                                ALU.subtract).then_inc(rest1, 1)
                    elif s[0] == "v":
                        use = vring[s]
                        wait(dve, v_full, b, NV, use + 1)
                        nc.vector.tensor_tensor(V1[:, s[1], :, 0:HD],
                                                vbank[use % 2][:, 0:H].rearrange("p (h d) -> p h d", d=HD),
                                                T["bv"][:].rearrange("p (h d) -> p h d", d=HD),
                                                ALU.add).then_inc(v_free, 1)
                    elif s[0] == "scores":
                        qb, k0, k1 = CHUNKS[s[3]]
                        use, row = vring[s], s[2] * TT + qb
                        bank = vbank[use % 2]
                        wait(dve, v_full, b, NV, use + 1)
                        if k1 < (qb + 1) * P:
                            nc.vector.tensor_reduce(MX[:, row, 2:3], bank[:, 0:512], AX.X, ALU.max).then_inc(v_free, 1)
                            continue
                        w = k1 - k0 - P
                        if w:
                            nc.vector.tensor_reduce(MX[:, row, 1:2], bank[:, 0:w], AX.X, ALU.max)
                        else:
                            nc.vector.memset(tick[:, use % 2:use % 2 + 1], 0.0)
                        nc.vector.tensor_tensor_reduce(out=junk[:, use % 2, :], in0=bank[:, w:w + P], in1=causal[:],
                                                       scale=1.0, scalar=LOWEST, op0=ALU.add, op1=ALU.max,
                                                       accum_out=MX[:, row, 0:1]).then_inc(v_free, 1)
                    elif s[0] == "maxima":
                        g = s[1]
                        wait(dve, v_free, b, NV, vring["scores", g, GH - 1, len(CHUNKS) - 1] + 1)
                        nc.vector.tensor_reduce(NM[:], MX[:], AX.X, ALU.max, negate=True).then_inc(maxima_done, 1)
                    elif s[0] == "max_rows":
                        g, use = s[1], vring[s]
                        src = vbank[use % 2][0:GH * TT, 0:P]
                        wait(dve, v_full, b, NV, use + 1)
                        wait(dve, rows_ready, b, NG * 48, g * 48)
                        nc.vector.tensor_copy(MT[:, 0, :], src).then_inc(mr1, 1)
                        wait(dve, mr1, b, NG, g + 1)
                        nc.vector.tensor_tensor(MR[:], src, MT[:, 0, :], ALU.subtract).then_inc(v_free, 1)
                        wait(dve, v_free, b, NV, use + 1)
                        nc.vector.tensor_copy(MT[:, 1, :], MR[:]).then_inc(mr2, 1)
                        wait(dve, mr2, b, NG, g + 1)
                        nc.vector.tensor_tensor(MT[:, 2, :], MR[:], MT[:, 1, :], ALU.subtract).then_inc(rows_split, 1)
                    elif s[0] == "heads_out":
                        g, half = s[1:]
                        n = 2 * g + half
                        wait(dve, values_done, b, NW, g * WSTEPS + (4 if half == 0 else WSTEPS))
                        nc.vector.transpose(OT[:], pv[:, :]).then_inc(pv_read, 1)
                        wait(dve, pv_read, b, NO, n + 1)
                        by_token = OT[:].rearrange("p (t d) -> p t d", d=32)
                        nc.vector.reciprocal(RC[:], by_token[:, :, HD]).then_inc(o_step, 1)
                        wait(dve, o_step, b, 2 * NO, 2 * n + 1)
                        nc.vector.tensor_tensor(by_token[:, :, 0:HD], by_token[:, :, 0:HD],
                                                RC[:].unsqueeze(2).to_broadcast([P, 16, HD]), ALU.mult).then_inc(o_step, 1)
                        wait(dve, o_step, b, 2 * NO, 2 * n + 2)
                        wait(dve, o_stored, b, NO * 16, n * 16)
                        nc.vector.transpose(OD[:], OT[:]).then_inc(o_ready, 1)
                        wait(dve, o_ready, b, NO, n + 1)
                    elif s[0] == "cube":
                        i = s[1]
                        wait(dve, squared, b, NI, i + 1)
                        nc.vector.scalar_tensor_tensor(out=A[:, i % 2, :], in0=A[:, i % 2, :], scalar=1.0, in1=G[:],
                                                       op0=ALU.add, op1=ALU.mult).then_inc(cubed, 1)
                    elif s[0] == "gelu":
                        i = s[1]
                        wait(dve, tanhed, b, NI, i + 1)
                        nc.vector.scalar_tensor_tensor(out=A[:, i % 2, :], in0=A[:, i % 2, :], scalar=1.0, in1=G[:],
                                                       op0=ALU.add, op1=ALU.mult).then_inc(gelued, 1)
                    elif s[0] == "unit":
                        u = s[1]
                        if u == 0:
                            wait(dve, bias_added, b, 1, 1)
                        wait(dve, down_done, b, NI, PAIRS * (u + 1))
                        nc.vector.tensor_tensor(res[:, 2 * u:2 * u + 2, :], acc[:, :].rearrange("p (t h) -> p t h", h=H),
                                                res[:, 2 * u:2 * u + 2, :], ALU.add).then_inc(acc_read, 1)
                    elif s[0] == "project":
                        j, use = s[1], vring[s]
                        if j == 0:
                            wait(dve, acc_read, b, NU, NU)
                        wait(dve, v_full, b, NV, use + 1)
                        nc.vector.tensor_tensor(res[:, j, :], vbank[use % 2][:, 0:H], res[:, j, :],
                                                ALU.add).then_inc(v_free, 1)
                        if j % 4 == 3:
                            wait(dve, v_free, b, NV, use + 1)
                            nc.vector.memset(tick[:, 2 + j // 4:3 + j // 4], 0.0).then_inc(finished, 4)

        @block.tensor
        def _(pe):
            pe.wait_ge(made, 5)

            def pair_product(dst, weights, i, nn):
                tokens = slice((i // PAIRS) * UNIT, (i // PAIRS + 1) * UNIT)
                n = 2 * (i % PAIRS) + nn
                for k in range(KT):
                    for p, (wp, xp) in enumerate(PASSES):
                        last = nc.tensor.matmul(dst[:, nn * UNIT:(nn + 1) * UNIT], weights[:, wp, k, n * P:(n + 1) * P],
                                                xT[:, xp, k, tokens], start=(k == 0 and p == 0),
                                                stop=(k == KT - 1 and p == 2))
                return last

            with pe.Fori(0, B) as b:
                for s in STEPS:
                    if s[0] in ("qk", "v", "scores", "max_rows", "project"):
                        use = vring[s]
                        dst = vbank[use % 2]
                        if s[0] == "max_rows":
                            wait(pe, maxima_done, b, NG, s[1] + 1)
                        wait(pe, v_free, b, NV, use - 1)
                        if s[0] == "qk":
                            m, which, c = qk_chunk(s[1])
                            col = which * H + m * P
                            for u in (2 * c, 2 * c + 1):
                                wait(pe, xt_ready[u], b, 16, 16)
                            for k in range(KT):
                                for p, (wp, xp) in enumerate(PASSES):
                                    last = nc.tensor.matmul(dst[:, :], WA[:, wp, k, col:col + P],
                                                            xT[:, xp, k, c * 512:(c + 1) * 512],
                                                            start=(k == 0 and p == 0), stop=(k == KT - 1 and p == 2))
                        elif s[0] == "v":
                            j = s[1]
                            for k in range(KT):
                                for p, (wp, xp) in enumerate(PASSES):
                                    last = nc.tensor.matmul(dst[:, 0:H], xT[:, xp, k, j * P:(j + 1) * P],
                                                            WA[:, wp, k, 2 * H:3 * H],
                                                            start=(k == 0 and p == 0), stop=(k == KT - 1 and p == 2))
                        elif s[0] == "scores":
                            g, h = s[1], s[2]
                            qb, k0, k1 = CHUNKS[s[3]]
                            if h % 2 == 0 and s[3] == 0:
                                wait(pe, staged[g % 2][h // 2], b, 64, 32 * (g // 2 + 1))
                            last = nc.tensor.matmul(dst[:, 0:k1 - k0], QS[0:KS_ROWS, g % 2, h, qb * P:(qb + 1) * P],
                                                    KS[0:KS_ROWS, g % 2, h, k0:k1], start=True, stop=True)
                        elif s[0] == "max_rows":
                            last = nc.tensor.transpose(dst[0:GH * TT, 0:P], NM[:], ident[:])
                        else:
                            j = s[1]
                            if j == 0:
                                wait(pe, packed, b, NH * 16, NH * 16)
                            for k in range(KT):
                                last = nc.tensor.matmul(dst[:, 0:H], OP[:, k, j * P:(j + 1) * P], WP[:, k, :],
                                                        start=(k == 0), stop=(k == KT - 1))
                        last.then_inc(v_full, 1)
                    elif s[0] == "weights":
                        g, t, h = s[1:]
                        use = wring[s]
                        half, j, off, diagonal = weight_step(t)
                        if t == 0 and h == 0:
                            wait(pe, rows_ready, b, NG * 48, (g + 1) * 48)
                        wait(pe, w_free, b, NWR, use - 1)
                        nc.tensor.matmul(wbank[use % 2][:, 0:512 - off], KS[0:KM_ROWS, g % 2, h, j * P:(j + 1) * P],
                                         QS[0:KM_ROWS, g % 2, h, half * 512 + off:(half + 1) * 512],
                                         start=True, stop=True).then_inc(w_full, 1)
                    elif s[0] == "values":
                        g, t = s[1:]
                        half, j, off, diagonal = weight_step(t)
                        if j == 0:
                            wait(pe, pv_read, b, NO, 2 * g + half)
                        if diagonal:
                            wait(pe, masked, b, ND, g * len(diagonals) + diagonals.index(t) + 1)
                        else:
                            wait(pe, w_free, b, NWR, wring["weights", g, t, GH - 1] + 1)
                        for h in range(GH):
                            last = nc.tensor.matmul(pv[32 * h:32 * h + HD + 1, off:512], V1[:, j, g * GH + h, :],
                                                    PR[:, t % 2, h, 0:512 - off], start=(j == 0),
                                                    stop=(t == 3 or t == WSTEPS - 1), tile_position=(0, 32 * h))
                        last.then_inc(values_done, 1)
                    elif s[0] == "gate":
                        i, nn = s[1:]
                        if nn == 0:
                            wait(pe, squared, b, NI, i)
                            if i % PAIRS == 0:
                                wait(pe, xt_ready[i // PAIRS], b, 16, 16)
                        last = pair_product(gate_b, WG, i, nn)
                        if nn:
                            last.then_inc(gate_full, 1)
                    elif s[0] == "up":
                        i, nn = s[1:]
                        if nn == 0:
                            wait(pe, up_copied, b, NI, i)
                        last = pair_product(up_b, WU, i, nn)
                        if nn:
                            last.then_inc(up_full, 1)
                    elif s[0] == "down":
                        i, nn = s[1:]
                        u, pair = i // PAIRS, i % PAIRS
                        if nn == 0:
                            if pair == 0:
                                wait(pe, acc_read, b, NU, u)
                            wait(pe, hi_done, b, NI, i + 1)
                            wait(pe, lo_done, b, NI, i + 1)
                        parts = (HI, LO)
                        for tt in range(2):
                            tokens = slice(nn * UNIT + tt * P, nn * UNIT + (tt + 1) * P)
                            for p, (wp, xp) in enumerate(PASSES):
                                last = nc.tensor.matmul(
                                    acc[:, tt * H:(tt + 1) * H], parts[xp][:, tokens], WD[:, wp, 2 * pair + nn, :],
                                    start=(pair == 0 and nn == 0 and tt == 0 and p == 0),
                                    stop=(pair == PAIRS - 1 and nn == 1 and p == 2), skip_group_check=True)
                        if nn:
                            last.then_inc(down_done, 1)


_INS = ["L0_attn_encodings", "L0_attn_w_attn", "L0_attn_b_attn", "L0_attn_w_proj", "L0_attn_b_proj",
        "L0_ffn_gate_W_packed", "L0_ffn_gate_scales", "L0_ffn_up_W_packed", "L0_ffn_up_scales",
        "L0_ffn_down_W_packed", "L0_ffn_down_scales"]


def kernel(**inputs):
    import numpy as _np
    import concourse.bacc as _bacc
    from concourse import mybir as _mybir
    from concourse.bass_utils import run_bass_kernel_spmd as _run

    nc = _bacc.Bacc("TRN2", target_bir_lowering=False, num_devices=1, dynamic_dma_scratch_size=1024)
    arrays, args = {}, []
    for name in _INS:
        a = _np.ascontiguousarray(inputs[name])
        arrays[f"in_{name}"] = a
        args.append(nc.dram_tensor(f"in_{name}", a.shape, _mybir.dt.from_np(a.dtype), kind="ExternalInput").ap())
    args.append(nc.dram_tensor("out_0", (B, S, H), _mybir.dt.float32, kind="ExternalOutput").ap())
    build(nc, *args)
    r = _run(nc, [arrays], core_ids=[0])
    return r.results[0]["out_0"]
```

```python
import concourse.bass as bass
from concourse import mybir
from contextlib import ExitStack

f32 = mybir.dt.float32
f32r = mybir.dt.float32r
bf16 = mybir.dt.bfloat16
i32 = mybir.dt.int32
fp8 = mybir.dt.float8e4
ALU = mybir.AluOpType
ACT = mybir.ActivationFunctionType
AX = mybir.AxisListType

P = 128
B, S, H = 4, 1024, 256
NH, HD = 16, 16
F = 2048
KT = H // P
NT = F // P
TT = S // P
UNIT = 256
NU = S // UNIT
PAIRS = NT // 2
NI = NU * PAIRS
GH = 4
NG = NH // GH
BLK = 32
RUNS_Q = ((0, 3, 0, True), (3, 2, 0, True), (5, 1, 0, True))
RUNS_K = ((0, 3, 0, False), (3, 2, 1, False), (5, 1, 2, False))
NTERM = 6
KS_ROWS = NTERM * HD
KM_ROWS = KS_ROWS + 3
LOWEST = -3.0e38
EPS = 1e-5
PASSES = ((0, 0), (0, 1), (1, 0))


def ffn_pieces():
    pieces = [[] for _ in range(PIECES)]
    for i in range(NI):
        for n, step in ((0, ("gate", i, 0)), (1, ("gate", i, 1)), (2, ("up", i, 0)), (3, ("up", i, 1)),
                        *zip(LAGS, [("square", i), ("cube", i), ("tanh", i), ("gelu", i),
                                    ("times_up", i), ("high", i), ("low", i), ("down", i, 0)]),
                        (LAGS[-1] + 1, ("down", i, 1))):
            pieces[6 * i + n].append(step)
        if i % PAIRS == PAIRS - 1:
            pieces[6 * i + 5].append(("refill", i // PAIRS))
            pieces[6 * i + LAGS[-1] + 2].append(("unit", i // PAIRS))
    return pieces


def sequence_steps():
    pieces = ffn_pieces()[::-1]
    steps = []

    def with_ffn(count, own):
        done = 0
        for n, step in enumerate(own):
            steps.extend(step)
            while done < count * (n + 1) // len(own):
                steps.extend(pieces.pop())
                done += 1

    def scores(g):
        return [("scores", g, h, n) for h in range(GH) for n in range(len(CHUNKS))]

    products = [("qk", 0), ("qk", 1), ("v", 0), ("qk", 2), ("v", 1), ("qk", 3), ("v", 2), ("v", 3),
                ("qk", 4), ("v", 4), ("qk", 5), ("v", 5), ("qk", 6), ("v", 6), ("qk", 7), ("v", 7)]
    own = [[p] for p in products]
    for n, p in enumerate(products):
        if p[0] == "qk":
            own[min(n + 1, len(own) - 1)].append(("qk_parts", p[1]))
    own[6] += [("stage", 0), ("stage", 1)]
    own[8].append(("load_x",))
    with_ffn(PIECES_QKV, own)
    own = [[s] for s in scores(0)]
    for j in range(TT):
        own[4 * j + 14].append(("bias", j))
    with_ffn(PIECES_SCORES, own)
    with_ffn(PIECES_MAXIMA, [[("maxima", 0)], [], [], [("max_rows", 0)], [], [], []])
    for g in range(NG):
        own = [[("weights", g, t, h)] for t in range(WSTEPS) for h in range(GH)]
        if g:
            own[MASK_AT].append(("mask", g - 1, WSTEPS - 1))
            own[GH - 1].append(("values", g - 1, WSTEPS - 1))
            for n, name in enumerate(HEADS_STEPS):
                own[GH + HEADS_AT + n].append((name, g - 1, 1))
        for t in range(1, WSTEPS):
            own[t * GH + MASK_AT].append(("mask", g, t - 1))
            own[t * GH + GH - 1].append(("values", g, t - 1))
        for n, name in enumerate(HEADS_STEPS):
            own[5 * GH + HEADS_AT + n].append((name, g, 0))
        if g < NG - 1:
            first, last = (0, AHEAD_LAST0) if g == 0 else (AHEAD_FIRST, AHEAD_LAST)
            for n, s in enumerate(scores(g + 1)):
                own[first + n * (last - first) // (GH * len(CHUNKS))].append(s)
            own[last].append(("maxima", g + 1))
            own[last + 2].append(("max_rows", g + 1))
            if g < NG - 2:
                own[-1].append(("stage", g + 2))
            else:
                own[-1] += [("fetch", 0), ("fetch", 1)]
        else:
            own[5 * GH].append(("fetch", NG - 2))
        with_ffn(PIECES_GROUP if g < NG - 1 else PIECES_LAST, own)
    steps += [("mask", NG - 1, WSTEPS - 1), ("values", NG - 1, WSTEPS - 1)]
    with_ffn(2, [[], []])
    steps += [(name, NG - 1, 1) for name in HEADS_STEPS] + [("fetch", NG - 1)]
    with_ffn(len(pieces) - 9, [[]])
    with_ffn(9, [[("project", j)] for j in range(TT - 2)])
    steps += [("project", j) for j in range(TT - 2, TT)]
    return steps


HEADS_STEPS = ("heads_by_token", "heads_sums", "heads_norm", "heads_out")
PIECES = 6 * NI + 7
MASK_AT = 0
LAGS = (2, 3, 4, 5, 6, 7, 8, 10) 
AHEAD_LAST0 = 34
AHEAD_FIRST = 8
AHEAD_LAST = 39
HEADS_AT = 0 
PIECES_QKV = 16
PIECES_SCORES = 30
PIECES_MAXIMA = 8
PIECES_GROUP = 35
PIECES_LAST = 19

CHUNKS = [(qb, k0, min(k0 + 512, (qb + 1) * P)) for qb in range(TT) for k0 in range(0, (qb + 1) * P, 512)]
WSTEPS = 12


def weight_step(t):
    half, j = (0, t) if t < 4 else (1, t - 4)
    diagonal = j >= 4 * half
    return half, j, P * (j - 4 * half) if diagonal else 0, diagonal


def build(nc, x_in, w_attn, b_attn, w_proj, b_proj, gate_w, gate_s, up_w, up_s, down_w, down_s, out):
    STEPS = sequence_steps()

    vring = {u: n for n, u in enumerate(u for u in STEPS if u[0] in ("qk", "v", "scores", "max_rows", "project"))}
    wring = {u: n for n, u in enumerate(u for u in STEPS if u[0] == "weights")}
    assert len(vring) % 2 == 0 and len(wring) % 2 == 0

    top = ExitStack()
    with top:
        def sb(name, shape, dt, where=None):
            return (where or top).enter_context(nc.sbuf_tensor(name, shape, dt))

        def sem(name, where=None):
            return (where or top).enter_context(nc.semaphore(name))

        WG = sb("WG", [P, 2, KT, F], f32r)
        WU = sb("WU", [P, 2, KT, F], f32r)
        WD = sb("WD", [P, 2, NT, H], f32r)
        WA = sb("WA", [P, 2, KT, 3 * H], f32r)
        WP = sb("WP", [P, KT, H], f32)
        bqk = sb("bqk", [P, 4], f32)
        bv = sb("bv", [P, H], f32)
        bp = sb("bp", [P, H], f32)
        KS = sb("KS", [P, 2, GH, S], bf16)
        V1 = sb("V1", [P, TT, NH, HD + 1], f32)
        ident = sb("ident", [P, P], f32)
        bqk_dram = nc.dram_tensor("bqk_by_dim", (4, P), f32, kind="Internal").ap()
        banks = [top.enter_context(nc.psum_tensor(f"bank{i}", [P, 512], f32)) for i in range(8)]
        qk_dram = nc.dram_tensor("qk_parts", (2, 2, NTERM, P, S), bf16, kind="Internal").ap()
        o_dram = nc.dram_tensor("head_outputs", (NG, P, S), f32, kind="Internal").ap()
        xn_dram = nc.dram_tensor("xn_parts", (B + 1, NU, P, 2, KT, UNIT), f32, kind="Internal").ap()

        setup_phase(nc, sem, sb, banks, locals())
        main_phase(nc, sem, sb, banks, locals(), STEPS, vring, wring)


def setup_steps(chunks):
    steps = [("codes", 0), ("codes", 1)]
    for b in range(B):
        steps.append(("norm", b))
        for c in range(chunks // B * b, chunks // B * (b + 1)):
            steps.append(("weights", c))
            if c % (chunks // B) == 0:
                steps.append(("x_low", b))
            if c + 2 < chunks:
                steps.append(("codes", c + 2))
            if c:
                steps.append(("w_low", c - 1))
        if b == 0:
            steps.append(("attn",))
    steps.append(("w_low", chunks - 1))
    return steps


def setup_phase(nc, sem, sb, banks, T):
    WG, WU, WD, WA, WP = T["WG"], T["WU"], T["WD"], T["WA"], T["WP"]
    ident, xn_dram = T["ident"], T["xn_dram"]
    NX = B * S // P
    NC = 12
    CW = 512
    STEPS = setup_steps(NC)
    with ExitStack() as own:
        X = sb("X", [P, NX, H], f32, own)
        stats = sb("stats", [P, NX, 6], f32, own)
        mv = sb("mv", [P, NX, 2], f32, own)
        rs = sb("rs", [P, 4, NX], f32, own)
        XS = sb("XS", [P, 2, 2, KT, 512], f32r, own)
        PK = sb("PK", [P, 2, CW], i32, own)
        CODE = sb("CODE", [P, 2, 4, CW], i32, own)
        WF = sb("WF", [P, 2, 2 * CW], f32, own)
        SC = sb("SC", [P, 3, P], f32, own)
        WT = sb("WT", [P, KT, 3 * H], f32, own)

        x_loaded = [sem(f"x_loaded{b}", own) for b in range(B)]
        wa_loaded, wp_loaded, bias_loaded, sc_loaded = (sem(n, own) for n in ("wa_loaded", "wp_loaded", "bias_loaded", "sc_loaded"))
        bias_ordered, spare_stored = sem("bias_ordered", own), sem("spare_stored", own)
        pk_loaded = [sem(f"pk_loaded{i}", own) for i in range(2)]
        consts_made = sem("consts_made", own)
        dve_step = sem("dve_step", own)
        var_ready, root_ready, xn_ready = (sem(n, own) for n in ("var_ready", "root_ready", "xn_ready"))
        xt_full, x_hi, x_lo = (sem(n, own) for n in ("xt_full", "x_hi", "x_lo"))
        xs_stored = [sem(f"xs_stored{i}", own) for i in range(2)]
        wa_hi, codes_apart, pairs_joined, codes_joined, wf_ready, wt_full, w_hi, w_lo = (
            sem(n, own) for n in ("wa_hi", "codes_apart", "pairs_joined", "codes_joined", "wf_ready", "wt_full", "w_hi", "w_lo"))
        block = own.enter_context(nc.Block())

        def packed(c):
            if c < 8:
                w = T["gate_w"] if c < 4 else T["up_w"]
                return w[(c % 4) * 512:(c % 4 + 1) * 512, :].rearrange("(i p) w -> p i w", p=P)
            c -= 8
            return T["down_w"][(c // 2) * P:(c // 2 + 1) * P, (c % 2) * CW:(c % 2 + 1) * CW]

        def attn_columns():
            for m in range(4):
                cols = slice(m * P, (m + 1) * P)
                yield WT[:, :, cols].rearrange("p k (h r) -> p k r h", h=8), cols
            yield WT[:, :, 2 * H:3 * H], slice(2 * H, 3 * H)

        def weight_dest(c, part, k):
            if c < 8:
                return (WG if c < 4 else WU)[:, part, k, (c % 4) * 512:(c % 4 + 1) * 512]
            c -= 8
            nt = (c % 2) * 8 + 4 * k
            return WD[:, part, nt:nt + 4, (c // 2) * P:(c // 2 + 1) * P]

        def bank_view(bank, c):
            return bank[:, :] if c < 8 else bank[:, :].rearrange("p (n h) -> p n h", h=P)

        @block.sync
        def _(sp):
            def load_packed(c):
                dst = PK[:, c % 2, :]
                if c < 8:
                    dst = dst.rearrange("p (i w) -> p i w", w=P)
                sp.dma_start(dst, packed(c)).then_inc(pk_loaded[c % 2], 16)

            load_packed(0)
            for b in range(B):
                sp.dma_start(X[:, b * TT:(b + 1) * TT, :],
                             T["x_in"][b].rearrange("(t p) h -> p t h", p=P)).then_inc(x_loaded[b], 16)
                if b == 0:
                    load_packed(1)
                    sp.dma_start(SC[:, 0, :].rearrange("p (t s) -> p t s", s=8),
                                 T["gate_s"].rearrange("(t p) s -> p t s", p=P)).then_inc(sc_loaded, 16)
                    sp.dma_start(SC[:, 1, :].rearrange("p (t s) -> p t s", s=8),
                                 T["up_s"].rearrange("(t p) s -> p t s", p=P)).then_inc(sc_loaded, 16)
                    sp.dma_start(SC[:, 2, :].rearrange("p (t s) -> p t s", s=64),
                                 T["down_s"].rearrange("(t p) s -> p t s", p=P)).then_inc(sc_loaded, 16)
                    sp.dma_start(WT[:], T["w_attn"].rearrange("(k p) n -> p k n", p=P)).then_inc(wa_loaded, 16)
                    sp.dma_start(WP[:], T["w_proj"].rearrange("(k p) n -> p k n", p=P)).then_inc(wp_loaded, 16)
                    for m in range(4):
                        sp.dma_start(T["bqk_dram"][m].rearrange("(r h) -> r h", h=8),
                                     T["b_attn"][m * P:(m + 1) * P].rearrange("(h r) -> r h", h=8),
                                     allow_slow_non_contiguous=True).then_inc(bias_ordered, 16)
                    sp.dma_start(T["bv"][:], T["b_attn"][2 * H:3 * H].partition_broadcast(P)).then_inc(bias_loaded, 16)
                    sp.dma_start(T["bp"][:], T["b_proj"].partition_broadcast(P)).then_inc(bias_loaded, 16)
            for s in STEPS:
                if s[0] == "codes" and s[1] + 2 < NC:
                    c = s[1]
                    sp.wait_ge(codes_apart, c + 1)
                    load_packed(c + 2)
                elif s[0] == "x_low":
                    for c in (2 * s[1], 2 * s[1] + 1):
                        sp.wait_ge(x_lo, 2 * c + 2)
                        for u in range(2):
                            sp.dma_start(xn_dram[c // 2, 2 * (c % 2) + u],
                                         XS[:, c % 2, :, :, u * UNIT:(u + 1) * UNIT].bitcast(f32)).then_inc(xs_stored[c % 2], 16)
            for u in range(NU):
                sp.dma_start(xn_dram[B, u], XS[:, 1, :, :, (u % 2) * UNIT:(u % 2 + 1) * UNIT].bitcast(f32)).then_inc(spare_stored, 16)
            sp.wait_ge(bias_ordered, 64)
            sp.dma_start(T["bqk"][:], T["bqk_dram"].rearrange("t p -> p t"),
                         allow_slow_non_contiguous=True).then_inc(bias_loaded, 16)
            for i in range(2):
                sp.wait_ge(xs_stored[i], 16 * B * S // 512)
            sp.wait_ge(spare_stored, 64)
            sp.wait_ge(wp_loaded, 16)
            sp.wait_ge(bias_loaded, 48)

        @block.gpsimd
        def _(pool):
            nc.gpsimd.memset(ident[:], 0.0).then_inc(consts_made, 1)
            pool.wait_ge(consts_made, 1)
            nc.gpsimd.affine_select(out=ident[:], in_=ident[:], compare_op=ALU.not_equal, fill=1.0, base=0,
                                    pattern=[[-1, P]], channel_multiplier=1).then_inc(consts_made, 1)
            nc.gpsimd.memset(T["V1"][:, :, :, HD:HD + 1], 1.0).then_inc(consts_made, 1)
            pool.wait_ge(consts_made, 3)
            nc.gpsimd.memset(T["KS"][KS_ROWS:P, :, :, :], 1.0).then_inc(consts_made, 1)
            pool.wait_ge(consts_made, 4)
            for s in STEPS:
                if s[0] == "codes":
                    c = s[1]
                    code = CODE[:, c % 2]
                    pool.wait_ge(codes_apart, c + 1)
                    nc.gpsimd.tensor_tensor(code[:, 0:2, :], code[:, 0:2, :], code[:, 2:4, :], ALU.add).then_inc(pairs_joined, 1)
                    pool.wait_ge(pairs_joined, c + 1)
                    nc.gpsimd.tensor_tensor(code[:, 0, :], code[:, 0, :], code[:, 1, :], ALU.add).then_inc(codes_joined, 1)

        @block.vector
        def _(dve):
            done = [0]

            def link(ins):
                ins.then_inc(dve_step, 1)
                done[0] += 1
                dve.wait_ge(dve_step, done[0])

            for s in STEPS:
                if s[0] == "codes":
                    c = s[1]
                    dve.wait_ge(pk_loaded[c % 2], 16 * (c // 2 + 1))
                    if c >= 2:
                        dve.wait_ge(wf_ready, c - 1)
                    for i, (shift, mask) in enumerate(((2, 0x1C), (4, 0x80), (6, 0x1C00), (8, 0x8000))):
                        last = nc.vector.tensor_scalar(CODE[:, c % 2, i, :], PK[:, c % 2, :], shift, mask,
                                                       ALU.logical_shift_left, ALU.bitwise_and)
                    last.then_inc(codes_apart, 1)
                elif s[0] == "norm":
                    b = s[1]
                    dve.wait_ge(x_loaded[b], 16)
                    own_tiles = slice(b * TT, (b + 1) * TT)
                    for t in range(b * TT, (b + 1) * TT):
                        last = nc.vector.bn_stats(stats[:, t, :], X[:, t, :])
                    link(last)
                    for t in range(b * TT, (b + 1) * TT):
                        last = nc.vector.bn_aggr(mv[:, t, :], stats[:, t, :])
                    link(last)
                    nc.vector.tensor_scalar(rs[:, 0, own_tiles], mv[:, own_tiles, 1], EPS, None,
                                            ALU.add).then_inc(var_ready, 1)
                    dve.wait_ge(var_ready, b + 1)
                    dve.wait_ge(root_ready, b + 1)
                    link(nc.vector.reciprocal(rs[:, 2, own_tiles], rs[:, 1, own_tiles]))
                    link(nc.vector.tensor_tensor(rs[:, 3, own_tiles], rs[:, 2, own_tiles], rs[:, 2, own_tiles], ALU.mult))
                    link(nc.vector.tensor_tensor(rs[:, 3, own_tiles], rs[:, 3, own_tiles], rs[:, 0, own_tiles], ALU.mult))
                    link(nc.vector.tensor_scalar(rs[:, 3, own_tiles], rs[:, 3, own_tiles], -0.5, 1.5, ALU.mult, ALU.add))
                    link(nc.vector.tensor_tensor(rs[:, 2, own_tiles], rs[:, 2, own_tiles], rs[:, 3, own_tiles], ALU.mult))
                    for t in range(b * TT, (b + 1) * TT):
                        nc.vector.tensor_scalar(X[:, t, :], X[:, t, :], mv[:, t, 0:1], rs[:, 2, t:t + 1],
                                                ALU.subtract, ALU.mult).then_inc(xn_ready, 1)
                elif s[0] == "x_low":
                    for c in (2 * s[1], 2 * s[1] + 1):
                        for k in range(KT):
                            dve.wait_ge(x_hi, 2 * c + k + 1)
                            if c >= 2:
                                dve.wait_ge(xs_stored[c % 2], 32 * (c // 2))
                            nc.vector.tensor_tensor(XS[:, c % 2, 1, k, :], banks[4 + 2 * (c % 2) + k][:, :],
                                                    XS[:, c % 2, 0, k, :].bitcast(f32), ALU.subtract).then_inc(x_lo, 1)
                elif s[0] == "weights":
                    c = s[1]
                    if c == 0:
                        dve.wait_ge(sc_loaded, 48)
                        nc.vector.tensor_scalar(SC[:, 0:2], SC[:, 0:2], 64.0, None, ALU.mult)
                        link(nc.vector.tensor_scalar(SC[:, 2], SC[:, 2], 32.0, None, ALU.mult))
                    dve.wait_ge(codes_joined, c + 1)
                    if c >= 2:
                        dve.wait_ge(wt_full, 2 * c - 2)
                    which, first = (c // 4, (c % 4) * 32) if c < 8 else (2, ((c - 8) // 2) * 64 + (c % 2) * 32)
                    scale = SC[:, which, first:first + 32].unsqueeze(2).unsqueeze(3).to_broadcast([P, 32, BLK // 2, 2])
                    code = CODE[:, c % 2, 0, :].bitcast(fp8).rearrange("p (b w c) -> p b w c", b=32, c=4)[:, :, :, 0:2]
                    nc.vector.tensor_tensor(WF[:, c % 2, :].rearrange("p (b w c) -> p b w c", b=32, c=2),
                                            code, scale, ALU.mult).then_inc(wf_ready, 1)
                elif s[0] == "w_low":
                    c = s[1]
                    for k in range(2):
                        dve.wait_ge(w_hi, 2 * c + k + 1)
                        nc.vector.tensor_tensor(weight_dest(c, 1, k), bank_view(banks[2 * (c % 2) + k], c),
                                                weight_dest(c, 0, k).bitcast(f32), ALU.subtract).then_inc(w_lo, 1)
                elif s[0] == "attn":
                    dve.wait_ge(wa_hi, 5)
                    for src, dst in attn_columns():
                        nc.vector.tensor_tensor(WA[:, 1, :, dst], src, WA[:, 0, :, dst].bitcast(f32), ALU.subtract)

        @block.scalar
        def _(act):
            for s in STEPS:
                if s[0] == "norm":
                    b = s[1]
                    own_tiles = slice(b * TT, (b + 1) * TT)
                    act.wait_ge(var_ready, b + 1)
                    nc.scalar.activation(rs[:, 1, own_tiles], rs[:, 0, own_tiles], ACT.Sqrt).then_inc(root_ready, 1)
                    for c in (2 * b, 2 * b + 1):
                        for k in range(KT):
                            act.wait_ge(xt_full, 2 * c + k + 1)
                            if c >= 2:
                                act.wait_ge(xs_stored[c % 2], 32 * (c // 2))
                            nc.scalar.activation(XS[:, c % 2, 0, k, :], banks[4 + 2 * (c % 2) + k][:, :],
                                                 ACT.Copy).then_inc(x_hi, 1)
                elif s[0] == "weights":
                    c = s[1]
                    for k in range(2):
                        act.wait_ge(wt_full, 2 * c + k + 1)
                        nc.scalar.activation(weight_dest(c, 0, k), bank_view(banks[2 * (c % 2) + k], c),
                                             ACT.Copy).then_inc(w_hi, 1)
                elif s[0] == "attn":
                    act.wait_ge(wa_loaded, 16)
                    for src, dst in attn_columns():
                        nc.scalar.activation(WA[:, 0, :, dst], src, ACT.Copy).then_inc(wa_hi, 1)

        @block.tensor
        def _(pe):
            pe.wait_ge(consts_made, 2)
            for s in STEPS:
                if s[0] == "norm":
                    for c in (2 * s[1], 2 * s[1] + 1):
                        for k in range(KT):
                            if c >= 2:
                                pe.wait_ge(x_lo, 2 * (c - 2) + k + 1)
                            for i in range(4):
                                t = 4 * c + i
                                pe.wait_ge(xn_ready, t + 1)
                                last = nc.tensor.transpose(banks[4 + 2 * (c % 2) + k][:, i * P:(i + 1) * P],
                                                           X[:, t, k * P:(k + 1) * P], ident[:])
                            last.then_inc(xt_full, 1)
                elif s[0] == "weights":
                    c = s[1]
                    pe.wait_ge(wf_ready, c + 1)
                    for k in range(2):
                        if c >= 2:
                            pe.wait_ge(w_lo, 2 * (c - 2) + k + 1)
                        for i in range(4):
                            col = (i * KT + k) * P if c < 8 else (4 * k + i) * P
                            last = nc.tensor.transpose(banks[2 * (c % 2) + k][:, i * P:(i + 1) * P],
                                                       WF[:, c % 2, col:col + P], ident[:])
                        last.then_inc(wt_full, 1)


def main_phase(nc, sem, sb, banks, T, STEPS, vring, wring):
    WG, WU, WD, WA, WP = T["WG"], T["WU"], T["WD"], T["WA"], T["WP"]
    KS, V1 = T["KS"], T["V1"]
    ident, xn_dram, qk_dram, o_dram = T["ident"], T["xn_dram"], T["qk_dram"], T["o_dram"]
    acc, gate_b, up_b, pv = banks[0], banks[1], banks[2], banks[3]
    vbank, wbank = banks[4:6], banks[6:8]
    with ExitStack() as own:
        xT = sb("xT", [P, 2, KT, S], f32r, own)
        res = sb("res", [P, TT, H], f32, own)
        QF = sb("QF", [P, 2, 512], f32, own)
        PT = sb("PT", [P, 2, 3, 512], bf16, own)
        QS = sb("QS", [P, 2, GH, S], bf16, own)
        causal = sb("causal", [P, 512], bf16, own)
        junk = QF[:].bitcast(bf16)
        tick = sb("tick", [P, 4], f32, own)
        carry = sb("carry", [1, WSTEPS + 1], f32, own)
        carried = sb("carried", [1, 8], f32, own)
        MX = sb("MX", [P, GH * TT, 2], f32, own)
        NM = sb("NM", [P, GH * TT], f32, own)
        MR = sb("MR", [GH * TT, P], f32, own)
        MT = sb("MT", [GH * TT, 3, P], bf16, own)
        PR = sb("PR", [P, 2, GH, 512], f32, own)
        OT = sb("OT", [P, 512], f32, own)
        RC = sb("RC", [P, 16], f32, own)
        OD = sb("OD", [P, 512], f32, own)
        A = sb("A", [P, 2, 512], f32, own)
        G = sb("G", [P, 512], f32, own)
        U = sb("U", [P, 512], f32, own)
        HI = sb("HI", [P, 512], f32r, own)
        LO = sb("LO", [P, 512], f32r, own)
        OP = QS[:, 0].rearrange("p h t -> p (h t)").bitcast(f32).rearrange("p (k t) -> p k t", k=KT)

        made, causal_clear = sem("made", own), sem("causal_clear", own)
        xt_ready = [sem(f"xt_ready{u}", own) for u in range(NU)]
        x_ready, bias_added = sem("x_ready", own), sem("bias_added", own)
        v_full, v_free, w_full, w_free = (sem(n, own) for n in ("v_full", "v_free", "w_full", "w_free"))
        part1, rest1, part2, part3 = (sem(n, own) for n in ("part1", "rest1", "part2", "part3"))
        spilled = [sem(f"spilled{m}", own) for m in range(2)]
        staged = [[sem(f"staged{m}_{h}", own) for h in range(2)] for m in range(2)]
        maxima_done, mr1, mr2, rows_split, rows_ready = (
            sem(n, own) for n in ("maxima_done", "mr1", "mr2", "rows_split", "rows_ready"))
        masked, values_done = sem("masked", own), sem("values_done", own)
        pv_read, o_step, o_ready, o_stored, packed = (
            sem(n, own) for n in ("pv_read", "o_step", "o_ready", "o_stored", "packed"))
        gate_full, up_full, gate_copied, squared, cubed, tanhed, up_copied, gelued, product, hi_done, lo_done = (
            sem(n, own) for n in ("gate_full", "up_full", "gate_copied", "squared", "cubed", "tanhed", "up_copied",
                                  "gelued", "product", "hi_done", "lo_done"))
        down_done, acc_read = sem("down_done", own), sem("acc_read", own)
        carried_out, finished, stored = sem("carried_out", own), sem("finished", own), sem("stored", own)
        counted = [x_ready, bias_added, v_full, v_free, w_full, w_free, part1, rest1, part2, part3, maxima_done, mr1,
                   mr2, rows_split, rows_ready, masked, values_done, pv_read, o_step, o_ready, o_stored, packed,
                   gate_full, up_full, gate_copied, squared, cubed, tanhed, up_copied, gelued, product, hi_done,
                   lo_done, down_done, acc_read, finished, stored, *xt_ready, *spilled, *staged[0], *staged[1]]
        block = own.enter_context(nc.Block())

        NQ, NW, NO = 8, NG * WSTEPS, NG * 2
        NV, NWR = len(vring), len(wring)
        diagonals = [t for t in range(WSTEPS) if weight_step(t)[3]]
        ND = NG * len(diagonals)
        SPILL = 3 * 16

        def wait(eng, s, b, per, k):
            eng.wait_ge(s, b * per + (max(k, 0) + 1))

        def qk_chunk(n):
            return n // 4, (n // 2) % 2, n % 2

        @block.sync
        def _(sp):
            for s in counted:
                sp.sem_inc(s, 1)
            sp.wait_ge(made, 4)

            def carrier(n):
                sp.dma_start(carried[:, n:n + 1], tick[0:1, 0:1]).then_inc(carried_out, 16)

            with sp.Fori(0, B) as b:
                for s in STEPS:
                    if s[0] == "qk_parts":
                        n = s[1]
                        m, which, c = qk_chunk(n)
                        wait(sp, part3, b, NQ, n + 1)
                        for first, count, part, changes in (RUNS_Q, RUNS_K)[which]:
                            src = (PT[:, n % 2, part:part + count, :] if changes else
                                   PT[:, n % 2, part:part + 1, :].to_broadcast([P, count, 512]))
                            dst = qk_dram[m, which, first:first + count, :, c * 512:(c + 1) * 512]
                            sp.dma_start(dst.rearrange("c p t -> p c t"), src).then_inc(spilled[n % 2], 16)
                    elif s[0] == "stage":
                        g = s[1]
                        m, first = g // 2, (g % 2) * GH
                        if g % 2 == 0:
                            wait(sp, spilled[0], b, 4 * SPILL, 2 * SPILL * (m + 1))
                            carrier(0)
                            wait(sp, spilled[1], b, 4 * SPILL, 2 * SPILL * (m + 1))
                            carrier(1)
                        if g > 1:
                            wait(sp, w_full, b, NWR, wring["weights", g - 2, WSTEPS - 1, GH - 1] + 1)
                        for h in (0, 2):
                            for which, dst in ((1, KS), (0, QS)):
                                src = qk_dram[m, which].rearrange("c (r h) t -> (c r) h t", h=8)
                                sp.dma_start(dst[0:KS_ROWS, g % 2, h:h + 2],
                                             src[:, first + h:first + h + 2]).then_inc(staged[g % 2][h // 2], 16)
                    elif s[0] == "max_rows":
                        g = s[1]
                        wait(sp, rows_split, b, NG, g + 1)
                        for c in range(3):
                            sp.dma_start(QS[KS_ROWS + c:KS_ROWS + c + 1, g % 2].rearrange("o h (q t) -> o (h q) t", t=P),
                                         MT[:, c, :]).then_inc(rows_ready, 16)
                    elif s[0] == "heads_out":
                        g, half = s[1], s[2]
                        wait(sp, o_ready, b, NO, 2 * g + half + 1)
                        sp.dma_start(o_dram[g, :, half * 512:(half + 1) * 512], OD[:]).then_inc(o_stored, 16)
                    elif s[0] == "fetch":
                        g = s[1]
                        wait(sp, o_stored, b, NO * 16, 32 * (g + 1))
                        if g == 0:
                            carrier(4)
                            wait(sp, w_full, b, NWR, wring["weights", NG - 2, WSTEPS - 1, GH - 1] + 1)
                        for h in range(GH):
                            row = ((g % 2) * GH + h) * HD
                            sp.dma_start(OP[row:row + HD, g // 2, :],
                                         o_dram[g, 32 * h:32 * h + HD, :]).then_inc(packed, 16)
                    elif s[0] == "project" and s[1] % 4 == 3:
                        j = s[1] - 3
                        wait(sp, finished, b, TT, j + 4)
                        carrier(2 + j // 4)
                        sp.dma_start(T["out"][b].rearrange("(t p) h -> p t h", p=P)[:, j:j + 4, :],
                                     res[:, j:j + 4, :]).then_inc(stored, 16)
            sp.wait_ge(stored, B * 32 + 1)
            sp.wait_ge(carried_out, B * 7 * 16)

        @block.gpsimd
        def _(pool):
            nc.gpsimd.memset(causal[:], 0.0).then_inc(causal_clear, 1)
            nc.gpsimd.memset(carry[:], 0.0).then_inc(made, 1)
            pool.wait_ge(causal_clear, 1)
            nc.gpsimd.affine_select(out=causal[:, 384:], in_=causal[:, 384:], compare_op=ALU.is_ge, fill=LOWEST, base=0,
                                    pattern=[[-1, P]], channel_multiplier=1).then_inc(made, 1)
            pool.wait_ge(made, 4)

            def carrier(n):
                nc.gpsimd.tensor_tensor(carry[:, n:n + 1], carry[:, WSTEPS:], carry[:, WSTEPS:], ALU.add)

            with pool.Fori(0, B) as b:
                for s in STEPS:
                    if s[0] == "qk_parts":
                        n = s[1]
                        wait(pool, part2, b, NQ, n + 1)
                        nc.gpsimd.tensor_tensor(PT[:, n % 2, 2, :], QF[:, n % 2], PT[:, n % 2, 1, :],
                                                ALU.subtract).then_inc(part3, 1)
                    elif s[0] == "bias":
                        wait(pool, x_ready, b, 16, 16)
                        nc.gpsimd.tensor_tensor(res[:, s[1], :], res[:, s[1], :], T["bp"][:],
                                                ALU.add).then_inc(bias_added, 1)
                    elif s[0] == "mask":
                        g, t = s[1:]
                        half, j, off, diagonal = weight_step(t)
                        if diagonal:
                            wait(pool, w_free, b, NWR, wring["weights", g, t, GH - 1] + 1)
                            carrier(t)
                            block_ = PR[:, t % 2, :, 0:P]
                            nc.gpsimd.affine_select(out=block_, in_=block_, compare_op=ALU.is_ge, fill=0.0, base=0,
                                                    pattern=[[0, GH], [1, P]], channel_multiplier=-1).then_inc(masked, 1)
                    elif s[0] == "times_up":
                        i = s[1]
                        wait(pool, gelued, b, NI, i + 1)
                        wait(pool, up_copied, b, NI, i + 1)
                        nc.gpsimd.tensor_tensor(A[:, i % 2, :], A[:, i % 2, :], U[:], ALU.mult).then_inc(product, 1)
                    elif s[0] == "low":
                        i = s[1]
                        wait(pool, hi_done, b, NI, i + 1)
                        nc.gpsimd.tensor_tensor(LO[:], A[:, i % 2, :], HI[:].bitcast(f32),
                                                ALU.subtract).then_inc(lo_done, 1)

        @block.scalar
        def _(act):
            def fill(u, b):
                act.dma_start(xT[:, :, :, u * UNIT:(u + 1) * UNIT].bitcast(f32), xn_dram[b, u]).then_inc(xt_ready[u], 16)

            for u in range(NU):
                fill(u, 0)
            act.wait_ge(made, 4)
            with act.Fori(0, B) as b:
                for s in STEPS:
                    if s[0] == "qk_parts":
                        n, use = s[1], vring["qk", s[1]]
                        wait(act, v_free, b, NV, use + 1)
                        wait(act, spilled[n % 2], b, 4 * SPILL, SPILL * (n // 2))
                        nc.scalar.activation(PT[:, n % 2, 0, :], QF[:, n % 2], ACT.Copy).then_inc(part1, 1)
                        wait(act, rest1, b, NQ, n + 1)
                        nc.scalar.activation(PT[:, n % 2, 1, :], QF[:, n % 2], ACT.Copy).then_inc(part2, 1)
                    elif s[0] == "load_x":
                        wait(act, stored, b, 32, 0)
                        act.dma_start(res[:], T["x_in"][b].rearrange("(t p) h -> p t h", p=P)).then_inc(x_ready, 16)
                    elif s[0] == "weights":
                        g, t, h = s[1:]
                        use = wring[s]
                        half, j, off, diagonal = weight_step(t)
                        if h == 0:
                            wait(act, values_done, b, NW, g * WSTEPS + t - 1)
                        wait(act, w_full, b, NWR, use + 1)
                        nc.scalar.activation(PR[:, t % 2, h, 0:512 - off], wbank[use % 2][:, 0:512 - off],
                                             ACT.Exp, scale=0.25).then_inc(w_free, 1)
                    elif s[0] == "square":
                        i = s[1]
                        wait(act, gate_full, b, NI, i + 1)
                        wait(act, gelued, b, NI, i)
                        nc.scalar.activation(G[:], gate_b[:, :], ACT.Copy).then_inc(gate_copied, 1)
                        wait(act, lo_done, b, NI, i - 1)
                        nc.scalar.activation(A[:, i % 2, :], gate_b[:, :], ACT.Square,
                                             scale=0.044715 ** 0.5).then_inc(squared, 1)
                    elif s[0] == "tanh":
                        i = s[1]
                        wait(act, up_full, b, NI, i + 1)
                        wait(act, product, b, NI, i)
                        nc.scalar.activation(U[:], up_b[:, :], ACT.Copy).then_inc(up_copied, 1)
                        wait(act, cubed, b, NI, i + 1)
                        nc.scalar.activation(A[:, i % 2, :], A[:, i % 2, :], ACT.Tanh,
                                             scale=0.7978845608028654).then_inc(tanhed, 1)
                    elif s[0] == "refill":
                        wait(act, up_full, b, NI, PAIRS * (s[1] + 1))
                        fill(s[1], b + 1)
                    elif s[0] == "high":
                        i = s[1]
                        wait(act, product, b, NI, i + 1)
                        wait(act, down_done, b, NI, i)
                        nc.scalar.activation(HI[:], A[:, i % 2, :], ACT.Copy).then_inc(hi_done, 1)
            for u in range(NU):
                act.wait_ge(xt_ready[u], 16 * (B + 1) + 1)

        @block.vector
        def _(dve):
            nc.vector.memset(pv[:, :], 0.0).then_inc(made, 1)
            nc.vector.memset(tick[:], 0.0)
            nc.vector.memset(MX[:], LOWEST).then_inc(made, 1)
            dve.wait_ge(made, 4)
            with dve.Fori(0, B) as b:
                for s in STEPS:
                    if s[0] == "qk":
                        n, use = s[1], vring[s]
                        m, which, c = qk_chunk(n)
                        wait(dve, part3, b, NQ, n - 1)
                        if n == 0:
                            wait(dve, v_free, b, NV, 0)
                        wait(dve, v_full, b, NV, use + 1)
                        nc.vector.tensor_scalar(QF[:, n % 2], vbank[use % 2][:, :],
                                                T["bqk"][:, 2 * which + m:2 * which + m + 1],
                                                None, ALU.add).then_inc(v_free, 1)
                    elif s[0] == "qk_parts":
                        n = s[1]
                        wait(dve, part1, b, NQ, n + 1)
                        nc.vector.tensor_tensor(QF[:, n % 2], QF[:, n % 2], PT[:, n % 2, 0, :],
                                                ALU.subtract).then_inc(rest1, 1)
                    elif s[0] == "v":
                        use = vring[s]
                        wait(dve, v_full, b, NV, use + 1)
                        nc.vector.tensor_tensor(V1[:, s[1], :, 0:HD],
                                                vbank[use % 2][:, 0:H].rearrange("p (h d) -> p h d", d=HD),
                                                T["bv"][:].rearrange("p (h d) -> p h d", d=HD),
                                                ALU.add).then_inc(v_free, 1)
                    elif s[0] == "scores":
                        qb, k0, k1 = CHUNKS[s[3]]
                        use, row = vring[s], s[2] * TT + qb
                        bank = vbank[use % 2]
                        if s[1:] == (0, 0, 0):
                            wait(dve, part3, b, NQ, NQ)
                        wait(dve, v_full, b, NV, use + 1)
                        w = k1 - k0
                        if k1 < (qb + 1) * P:
                            nc.vector.tensor_reduce(MX[:, row, 1:2], bank[:, 0:w], AX.X, ALU.max).then_inc(v_free, 1)
                        else:
                            nc.vector.memset(tick[:, use % 2:use % 2 + 1], 0.0)
                            nc.vector.tensor_tensor_reduce(out=junk[:, use % 2, 0:w], in0=bank[:, 0:w],
                                                           in1=causal[:, 512 - w:], scale=1.0, scalar=LOWEST,
                                                           op0=ALU.add, op1=ALU.max,
                                                           accum_out=MX[:, row, 0:1]).then_inc(v_free, 1)
                    elif s[0] == "maxima":
                        g = s[1]
                        wait(dve, v_free, b, NV, vring["scores", g, GH - 1, len(CHUNKS) - 1] + 1)
                        nc.vector.tensor_reduce(NM[:], MX[:], AX.X, ALU.max, negate=True).then_inc(maxima_done, 1)
                    elif s[0] == "max_rows":
                        g, use = s[1], vring[s]
                        src = vbank[use % 2][0:GH * TT, 0:P]
                        wait(dve, v_full, b, NV, use + 1)
                        wait(dve, rows_ready, b, NG * 48, g * 48)
                        nc.vector.tensor_copy(MT[:, 0, :], src).then_inc(mr1, 1)
                        wait(dve, mr1, b, NG, g + 1)
                        nc.vector.tensor_tensor(MR[:], src, MT[:, 0, :], ALU.subtract).then_inc(v_free, 1)
                        wait(dve, v_free, b, NV, use + 1)
                        nc.vector.tensor_copy(MT[:, 1, :], MR[:]).then_inc(mr2, 1)
                        wait(dve, mr2, b, NG, g + 1)
                        nc.vector.tensor_tensor(MT[:, 2, :], MR[:], MT[:, 1, :], ALU.subtract).then_inc(rows_split, 1)
                    elif s[0] in HEADS_STEPS:
                        g, half = s[1:]
                        n = 2 * g + half
                        by_token = OT[:].rearrange("p (t d) -> p t d", d=32)
                        if s[0] == "heads_by_token":
                            wait(dve, o_ready, b, NO, n)
                            wait(dve, values_done, b, NW, g * WSTEPS + (4 if half == 0 else WSTEPS))
                            nc.vector.transpose(OT[:], pv[:, :]).then_inc(pv_read, 1)
                        elif s[0] == "heads_sums":
                            wait(dve, pv_read, b, NO, n + 1)
                            nc.vector.reciprocal(RC[:], by_token[:, :, HD]).then_inc(o_step, 1)
                        elif s[0] == "heads_norm":
                            wait(dve, o_step, b, 2 * NO, 2 * n + 1)
                            nc.vector.tensor_tensor(by_token[:, :, 0:HD], by_token[:, :, 0:HD],
                                                    RC[:].unsqueeze(2).to_broadcast([P, 16, HD]),
                                                    ALU.mult).then_inc(o_step, 1)
                        else:
                            wait(dve, o_step, b, 2 * NO, 2 * n + 2)
                            wait(dve, o_stored, b, NO * 16, n * 16)
                            nc.vector.transpose(OD[:], OT[:]).then_inc(o_ready, 1)
                    elif s[0] == "cube":
                        i = s[1]
                        wait(dve, squared, b, NI, i + 1)
                        nc.vector.scalar_tensor_tensor(out=A[:, i % 2, :], in0=A[:, i % 2, :], scalar=1.0, in1=G[:],
                                                       op0=ALU.add, op1=ALU.mult).then_inc(cubed, 1)
                    elif s[0] == "gelu":
                        i = s[1]
                        wait(dve, tanhed, b, NI, i + 1)
                        nc.vector.scalar_tensor_tensor(out=A[:, i % 2, :], in0=A[:, i % 2, :], scalar=1.0, in1=G[:],
                                                       op0=ALU.add, op1=ALU.mult).then_inc(gelued, 1)
                    elif s[0] == "unit":
                        u = s[1]
                        wait(dve, bias_added, b, TT, 2 * u + 2)
                        wait(dve, down_done, b, NI, PAIRS * (u + 1))
                        nc.vector.tensor_tensor(res[:, 2 * u:2 * u + 2, :], acc[:, :].rearrange("p (t h) -> p t h", h=H),
                                                res[:, 2 * u:2 * u + 2, :], ALU.add).then_inc(acc_read, 1)
                    elif s[0] == "project":
                        j, use = s[1], vring[s]
                        if j % 2 == 0:
                            wait(dve, acc_read, b, NU, j // 2 + 1)
                        wait(dve, v_full, b, NV, use + 1)
                        nc.vector.tensor_tensor(res[:, j, :], vbank[use % 2][:, 0:H], res[:, j, :],
                                                ALU.add).then_inc(v_free, 1)
                        if j % 4 == 3:
                            wait(dve, v_free, b, NV, use + 1)
                            nc.vector.memset(tick[:, 2 + j // 4:3 + j // 4], 0.0).then_inc(finished, 4)

        @block.tensor
        def _(pe):
            pe.wait_ge(made, 4)

            def pair_product(dst, weights, i, nn):
                tokens = slice((i // PAIRS) * UNIT, (i // PAIRS + 1) * UNIT)
                n = 2 * (i % PAIRS) + nn
                for k in range(KT):
                    for p, (wp, xp) in enumerate(PASSES):
                        last = nc.tensor.matmul(dst[:, nn * UNIT:(nn + 1) * UNIT], weights[:, wp, k, n * P:(n + 1) * P],
                                                xT[:, xp, k, tokens], start=(k == 0 and p == 0),
                                                stop=(k == KT - 1 and p == 2))
                return last

            with pe.Fori(0, B) as b:
                for s in STEPS:
                    if s[0] in ("qk", "v", "scores", "max_rows", "project"):
                        use = vring[s]
                        dst = vbank[use % 2]
                        if s[0] == "max_rows":
                            wait(pe, maxima_done, b, NG, s[1] + 1)
                        wait(pe, v_free, b, NV, use - 1)
                        if s[0] == "qk":
                            m, which, c = qk_chunk(s[1])
                            col = which * H + m * P
                            for u in (2 * c, 2 * c + 1):
                                wait(pe, xt_ready[u], b, 16, 16)
                            for k in range(KT):
                                for p, (wp, xp) in enumerate(PASSES):
                                    last = nc.tensor.matmul(dst[:, :], WA[:, wp, k, col:col + P],
                                                            xT[:, xp, k, c * 512:(c + 1) * 512],
                                                            start=(k == 0 and p == 0), stop=(k == KT - 1 and p == 2))
                        elif s[0] == "v":
                            j = s[1]
                            for k in range(KT):
                                for p, (wp, xp) in enumerate(PASSES):
                                    last = nc.tensor.matmul(dst[:, 0:H], xT[:, xp, k, j * P:(j + 1) * P],
                                                            WA[:, wp, k, 2 * H:3 * H],
                                                            start=(k == 0 and p == 0), stop=(k == KT - 1 and p == 2))
                        elif s[0] == "scores":
                            g, h = s[1], s[2]
                            qb, k0, k1 = CHUNKS[s[3]]
                            if h % 2 == 0 and s[3] == 0:
                                wait(pe, staged[g % 2][h // 2], b, 64, 32 * (g // 2 + 1))
                            last = nc.tensor.matmul(dst[:, 0:k1 - k0], QS[0:KS_ROWS, g % 2, h, qb * P:(qb + 1) * P],
                                                    KS[0:KS_ROWS, g % 2, h, k0:k1], start=True, stop=True)
                        elif s[0] == "max_rows":
                            last = nc.tensor.transpose(dst[0:GH * TT, 0:P], NM[:], ident[:])
                        else:
                            j = s[1]
                            if j == 0:
                                wait(pe, packed, b, NH * 16, NH * 16)
                            for k in range(KT):
                                last = nc.tensor.matmul(dst[:, 0:H], OP[:, k, j * P:(j + 1) * P], WP[:, k, :],
                                                        start=(k == 0), stop=(k == KT - 1))
                        last.then_inc(v_full, 1)
                    elif s[0] == "weights":
                        g, t, h = s[1:]
                        use = wring[s]
                        half, j, off, diagonal = weight_step(t)
                        if t == 0 and h == 0:
                            wait(pe, rows_ready, b, NG * 48, (g + 1) * 48)
                        wait(pe, w_free, b, NWR, use - 1)
                        nc.tensor.matmul(wbank[use % 2][:, 0:512 - off], KS[0:KM_ROWS, g % 2, h, j * P:(j + 1) * P],
                                         QS[0:KM_ROWS, g % 2, h, half * 512 + off:(half + 1) * 512],
                                         start=True, stop=True).then_inc(w_full, 1)
                    elif s[0] == "values":
                        g, t = s[1:]
                        half, j, off, diagonal = weight_step(t)
                        if j == 0:
                            wait(pe, pv_read, b, NO, 2 * g + half)
                        if diagonal:
                            wait(pe, masked, b, ND, g * len(diagonals) + diagonals.index(t) + 1)
                        else:
                            wait(pe, w_free, b, NWR, wring["weights", g, t, GH - 1] + 1)
                        for h in range(GH):
                            last = nc.tensor.matmul(pv[32 * h:32 * h + HD + 1, off:512], V1[:, j, g * GH + h, :],
                                                    PR[:, t % 2, h, 0:512 - off], start=(j == 0),
                                                    stop=(t == 3 or t == WSTEPS - 1), tile_position=(0, 32 * h))
                        last.then_inc(values_done, 1)
                    elif s[0] == "gate":
                        i, nn = s[1:]
                        if nn == 0:
                            wait(pe, squared, b, NI, i)
                            if i % PAIRS == 0:
                                wait(pe, xt_ready[i // PAIRS], b, 16, 16)
                        last = pair_product(gate_b, WG, i, nn)
                        if nn:
                            last.then_inc(gate_full, 1)
                    elif s[0] == "up":
                        i, nn = s[1:]
                        if nn == 0:
                            wait(pe, up_copied, b, NI, i)
                        last = pair_product(up_b, WU, i, nn)
                        if nn:
                            last.then_inc(up_full, 1)
                    elif s[0] == "down":
                        i, nn = s[1:]
                        u, pair = i // PAIRS, i % PAIRS
                        if nn == 0:
                            if pair == 0:
                                wait(pe, acc_read, b, NU, u)
                            wait(pe, hi_done, b, NI, i + 1)
                            wait(pe, lo_done, b, NI, i + 1)
                        parts = (HI, LO)
                        for tt in range(2):
                            tokens = slice(nn * UNIT + tt * P, nn * UNIT + (tt + 1) * P)
                            for p, (wp, xp) in enumerate(PASSES):
                                last = nc.tensor.matmul(
                                    acc[:, tt * H:(tt + 1) * H], parts[xp][:, tokens], WD[:, wp, 2 * pair + nn, :],
                                    start=(pair == 0 and nn == 0 and tt == 0 and p == 0),
                                    stop=(pair == PAIRS - 1 and nn == 1 and p == 2), skip_group_check=True)
                        if nn:
                            last.then_inc(down_done, 1)


_INS = ["L0_attn_encodings", "L0_attn_w_attn", "L0_attn_b_attn", "L0_attn_w_proj", "L0_attn_b_proj",
        "L0_ffn_gate_W_packed", "L0_ffn_gate_scales", "L0_ffn_up_W_packed", "L0_ffn_up_scales",
        "L0_ffn_down_W_packed", "L0_ffn_down_scales"]


def kernel(**inputs):
    import numpy as _np
    import concourse.bacc as _bacc
    from concourse import mybir as _mybir
    from concourse.bass_utils import run_bass_kernel_spmd as _run

    nc = _bacc.Bacc("TRN2", target_bir_lowering=False, num_devices=1, dynamic_dma_scratch_size=1024)
    arrays, args = {}, []
    for name in _INS:
        a = _np.ascontiguousarray(inputs[name])
        arrays[f"in_{name}"] = a
        args.append(nc.dram_tensor(f"in_{name}", a.shape, _mybir.dt.from_np(a.dtype), kind="ExternalInput").ap())
    args.append(nc.dram_tensor("out_0", (B, S, H), _mybir.dt.float32, kind="ExternalOutput").ap())
    build(nc, *args)
    r = _run(nc, [arrays], core_ids=[0])
    return r.results[0]["out_0"]
```
